# Optimizing a Trainium2 kernel written in Bass

```python
import numpy as np
import jax
import jax.numpy as jnp

def _softmax(x, axis=-1):
    return jax.nn.softmax(x, axis=axis)

def _gelu(x):
    return jax.nn.gelu(x, approximate=True)

def _silu(x):
    return jax.nn.silu(x)

def _sigmoid(x):
    return jax.nn.sigmoid(x)

def _layernorm(x, axis=-1, eps=1e-05):
    m = jnp.mean(x, axis=axis, keepdims=True)
    v = jnp.var(x, axis=axis, keepdims=True)
    return (x - m) / jnp.sqrt(v + eps)

def _scatter_add(tgt, idx, src, axis=0):
    return tgt.at[idx].add(src)

def _segment_sum(src, seg, n):
    return jax.ops.segment_sum(src, seg, n)
kernel_name = 'mk_cond_seq_d4_seqx_r8_d79654'

def setup_inputs(seed: int=0):
    np.random.seed(seed)
    _w = jnp.asarray

    def _rec_inputs():
        import jax
        import jax.numpy as jnp
        _rk = jax.random.key(seed)
        x = 0.5 + 0.2887 * jax.random.normal(jax.random.fold_in(_rk, 1), (32, 32, 128), jnp.float32)
        _lenS = 32 - jax.random.randint(jax.random.fold_in(_rk, 7), (32,), 0, max(1, 32 // 4) + 1, jnp.int32)
        _lenS2 = 32 - jax.random.randint(jax.random.fold_in(_rk, 8), (32,), 0, max(1, 32 // 4) + 1, jnp.int32)
        cond_1024 = jax.random.uniform(jax.random.fold_in(_rk, 11), (32, 128), jnp.float32, 0.0, 0.999994)
        _validS = jnp.arange(32)[None, :] < _lenS[:, None]
        _validS2 = jnp.arange(32)[None, :] < _lenS2[:, None]
        _causal = jnp.tril(jnp.ones((32, 32), dtype=bool))
        mask_BxSxSx11_ik0 = jnp.where(jnp.ones((32, 32, 32, 11), dtype=bool), 0, 1).astype(jnp.int32)
        return (x, cond_1024, mask_BxSxSx11_ik0)
    x, cond_1024, mask_BxSxSx11_ik0 = _rec_inputs()

    def _L0_cond_setup():
        import jax, jax.numpy as jnp
        import numpy as np
        N, HW, C = (32, 512, 128)
        WRS_RATIO = 0.5
        P = 0.9
        M = int(WRS_RATIO * C)
        key = jax.random.key(seed)
        k1, k2, k3 = jax.random.split(key, 3)
        x = jax.random.uniform(k1, (N, HW, C), dtype=jnp.float32)
        r = jax.random.uniform(k2, (N, C), dtype=jnp.float32)
        u = jax.random.uniform(k3, (N, C), dtype=jnp.float32)
        return {'x': x, 'r': r, 'u': u}
    _L0_cond_all = _L0_cond_setup()
    _L0_cond_in = {k: v for k, v in _L0_cond_all.items() if k in ()}
    del _L0_cond_all

    def _L1_cond_setup():
        import jax, jax.numpy as jnp
        import numpy as np
        H = 128
        NH = 16
        DH = H // NH
        MLP = 4 * H
        EPS = 1e-05

        def _ln(x):
            m = jnp.mean(x, axis=-1, keepdims=True)
            v = jnp.mean((x - m) ** 2, axis=-1, keepdims=True)
            return (x - m) * jax.lax.rsqrt(v + EPS)

        def _modulate(x, shift, scale):
            return x * (1.0 + scale[:, None, :]) + shift[:, None, :]
        key = jax.random.key(seed)
        ks = jax.random.split(key, 12)
        s = 1.0 / np.sqrt(H)
        inp = {'x': jax.random.normal(ks[0], (8, 128, H), jnp.float32), 'c': jax.random.normal(ks[1], (8, H), jnp.float32), 'Wc': jax.random.normal(ks[2], (H, 6 * H), jnp.float32) * s, 'bc': jnp.zeros((6 * H,), jnp.float32), 'Wq': jax.random.normal(ks[3], (H, H), jnp.float32) * s, 'bq': jnp.zeros((H,), jnp.float32), 'Wk': jax.random.normal(ks[4], (H, H), jnp.float32) * s, 'bk': jnp.zeros((H,), jnp.float32), 'Wv': jax.random.normal(ks[5], (H, H), jnp.float32) * s, 'bv': jnp.zeros((H,), jnp.float32), 'Wo': jax.random.normal(ks[6], (H, H), jnp.float32) * s, 'bo': jnp.zeros((H,), jnp.float32), 'W1': jax.random.normal(ks[7], (H, MLP), jnp.float32) * s, 'b1': jnp.zeros((MLP,), jnp.float32), 'W2': jax.random.normal(ks[8], (MLP, H), jnp.float32) * (1.0 / np.sqrt(MLP)), 'b2': jnp.zeros((H,), jnp.float32)}
        return inp
    _L1_cond_all = _L1_cond_setup()
    _L1_cond_in = {k: v for k, v in _L1_cond_all.items() if k in ('Wc', 'bc', 'Wq', 'bq', 'Wk', 'bk', 'Wv', 'bv', 'Wo', 'bo', 'W1', 'b1', 'W2', 'b2')}
    del _L1_cond_all

    def _L2_cond_setup():
        import jax, jax.numpy as jnp
        import numpy as np
        NONGT = 20
        H = 16
        NEG = -9000000000000000.0

        def _gat_attention(self_feat, cond_adj, label_bias, Wq, bq, Wk, bk, Wout, bout):
            B, N, F = self_feat.shape
            ng = min(NONGT, N)
            dh = F // H
            kv = self_feat[:, :ng]
            qh = (self_feat @ Wq.T + bq).reshape(B, N, H, dh)
            kh = (kv @ Wk.T + bk).reshape(B, ng, H, dh)
            aff = jnp.einsum('bnhd,bmhd->bnhm', qh, kh) * (1.0 / np.sqrt(dh))
            mask = cond_adj[:, :, None, :] > 0
            aff = jnp.where(mask, aff, NEG) + label_bias[:, :, None, :]
            w = jax.nn.softmax(aff, axis=-1)
            out_t = jnp.einsum('bnhm,bmf->bnhf', w, kv)
            out = jnp.einsum('bnhf,hgf->bnhg', out_t, Wout) + bout.reshape(H, F // H)
            return out.reshape(B, N, F)

        def _forward(v, q, adj, W_self, b_self, w_bias, b_bias, Wq, bq, Wk, bk, Wout, bout):
            adj_f = adj.astype(jnp.float32)
            exp_v = v
            row_zero = exp_v.sum(-1) == 0
            q_exp = jnp.where(row_zero[..., None], 0.0, q[:, None, :])
            vcq = jnp.concatenate([exp_v, q_exp], axis=-1)
            self_feat = vcq @ W_self.T + b_self
            output = self_feat
            for d in range(2):
                A = adj_f if d == 0 else jnp.swapaxes(adj_f, 1, 2)
                A = A[:, :, :NONGT, :]
                cond = A.sum(-1)
                vb = A @ w_bias + b_bias
                output = output + _gat_attention(self_feat, cond, vb, Wq[d], bq[d], Wk[d], bk[d], Wout[d], bout[d])
            rel = jax.nn.relu(output)
            return exp_v + rel
        key = jax.random.key(seed)
        ks = jax.random.split(key, 8)
        B, N, L, F, Q = (32, 36, 11, 128, 128)
        IN = F + Q
        s = 0.02
        return {'v': jax.random.normal(ks[0], (B, N, F), jnp.float32), 'q': jax.random.normal(ks[1], (B, Q), jnp.float32), 'adj': jax.random.randint(ks[2], (B, N, N, L), 0, 2, jnp.int32), 'W_self': jax.random.normal(ks[3], (F, IN), jnp.float32) * s, 'b_self': jnp.zeros((F,), jnp.float32), 'w_bias': jax.random.normal(ks[4], (L,), jnp.float32) * s, 'b_bias': jnp.zeros((), jnp.float32), 'Wq': jax.random.normal(ks[5], (2, F, F), jnp.float32) * s, 'bq': jnp.zeros((2, F), jnp.float32), 'Wk': jax.random.normal(ks[6], (2, F, F), jnp.float32) * s, 'bk': jnp.zeros((2, F), jnp.float32), 'Wout': jax.random.normal(ks[7], (2, H, F // H, F), jnp.float32) * s, 'bout': jnp.zeros((2, F), jnp.float32)}
    _L2_cond_all = _L2_cond_setup()
    _L2_cond_in = {k: v for k, v in _L2_cond_all.items() if k in ('W_self', 'b_self', 'w_bias', 'b_bias', 'Wq', 'bq', 'Wk', 'bk', 'Wout', 'bout')}
    del _L2_cond_all

    def _L3_cond_setup():
        import jax, jax.numpy as jnp
        import numpy as np
        DIM = 128
        MLP_RATIO = 4
        EPS = 1e-06

        def rmsnorm(x, w):
            return x * jax.lax.rsqrt(jnp.mean(x * x, axis=-1, keepdims=True) + EPS) * w

        def film(x, cond, w, b):
            ss = cond @ w + b
            scale, shift = jnp.split(ss, 2, axis=-1)
            return x * (1.0 + scale[:, None, :]) + shift[:, None, :]
        key = jax.random.key(seed)
        ks = jax.random.split(key, 16)
        B, N, D = (4, 256, DIM)
        H = D * MLP_RATIO
        s = lambda fan_in: 1.0 / np.sqrt(fan_in)
        return {'x': jax.random.normal(ks[0], (B, N, D), jnp.float32), 'cond': jax.random.normal(ks[1], (B, D), jnp.float32), 'norm1_w': jnp.ones((D,), jnp.float32), 'film1_w': jax.random.normal(ks[2], (D, 2 * D), jnp.float32) * s(D), 'film1_b': jnp.zeros((2 * D,), jnp.float32), 'q_w': jax.random.normal(ks[3], (D, D), jnp.float32) * s(D), 'q_b': jnp.zeros((D,), jnp.float32), 'k_w': jax.random.normal(ks[4], (D, D), jnp.float32) * s(D), 'k_b': jnp.zeros((D,), jnp.float32), 'v_w': jax.random.normal(ks[5], (D, D), jnp.float32) * s(D), 'v_b': jnp.zeros((D,), jnp.float32), 'proj_w': jax.random.normal(ks[6], (D, D), jnp.float32) * s(D), 'proj_b': jnp.zeros((D,), jnp.float32), 'norm2_w': jnp.ones((D,), jnp.float32), 'film2_w': jax.random.normal(ks[7], (D, 2 * D), jnp.float32) * s(D), 'film2_b': jnp.zeros((2 * D,), jnp.float32), 'mlp_w1': jax.random.normal(ks[8], (D, H), jnp.float32) * s(D), 'mlp_b1': jnp.zeros((H,), jnp.float32), 'mlp_w2': jax.random.normal(ks[9], (H, D), jnp.float32) * s(H), 'mlp_b2': jnp.zeros((D,), jnp.float32)}
    _L3_cond_all = _L3_cond_setup()
    _L3_cond_in = {k: v for k, v in _L3_cond_all.items() if k in ('norm1_w', 'film1_w', 'film1_b', 'q_w', 'q_b', 'k_w', 'k_b', 'v_w', 'v_b', 'proj_w', 'proj_b', 'norm2_w', 'film2_w', 'film2_b', 'mlp_w1', 'mlp_b1', 'mlp_w2', 'mlp_b2')}
    del _L3_cond_all
    return {'x': x, 'cond_1024': cond_1024, 'mask_BxSxSx11_ik0': mask_BxSxSx11_ik0, 'L1_cond_Wc': _L1_cond_in['Wc'], 'L1_cond_bc': _L1_cond_in['bc'], 'L1_cond_Wq': _L1_cond_in['Wq'], 'L1_cond_bq': _L1_cond_in['bq'], 'L1_cond_Wk': _L1_cond_in['Wk'], 'L1_cond_bk': _L1_cond_in['bk'], 'L1_cond_Wv': _L1_cond_in['Wv'], 'L1_cond_bv': _L1_cond_in['bv'], 'L1_cond_Wo': _L1_cond_in['Wo'], 'L1_cond_bo': _L1_cond_in['bo'], 'L1_cond_W1': _L1_cond_in['W1'], 'L1_cond_b1': _L1_cond_in['b1'], 'L1_cond_W2': _L1_cond_in['W2'], 'L1_cond_b2': _L1_cond_in['b2'], 'L2_cond_W_self': _L2_cond_in['W_self'], 'L2_cond_b_self': _L2_cond_in['b_self'], 'L2_cond_w_bias': _L2_cond_in['w_bias'], 'L2_cond_b_bias': _L2_cond_in['b_bias'], 'L2_cond_Wq': _L2_cond_in['Wq'], 'L2_cond_bq': _L2_cond_in['bq'], 'L2_cond_Wk': _L2_cond_in['Wk'], 'L2_cond_bk': _L2_cond_in['bk'], 'L2_cond_Wout': _L2_cond_in['Wout'], 'L2_cond_bout': _L2_cond_in['bout'], 'L3_cond_norm1_w': _L3_cond_in['norm1_w'], 'L3_cond_film1_w': _L3_cond_in['film1_w'], 'L3_cond_film1_b': _L3_cond_in['film1_b'], 'L3_cond_q_w': _L3_cond_in['q_w'], 'L3_cond_q_b': _L3_cond_in['q_b'], 'L3_cond_k_w': _L3_cond_in['k_w'], 'L3_cond_k_b': _L3_cond_in['k_b'], 'L3_cond_v_w': _L3_cond_in['v_w'], 'L3_cond_v_b': _L3_cond_in['v_b'], 'L3_cond_proj_w': _L3_cond_in['proj_w'], 'L3_cond_proj_b': _L3_cond_in['proj_b'], 'L3_cond_norm2_w': _L3_cond_in['norm2_w'], 'L3_cond_film2_w': _L3_cond_in['film2_w'], 'L3_cond_film2_b': _L3_cond_in['film2_b'], 'L3_cond_mlp_w1': _L3_cond_in['mlp_w1'], 'L3_cond_mlp_b1': _L3_cond_in['mlp_b1'], 'L3_cond_mlp_w2': _L3_cond_in['mlp_w2'], 'L3_cond_mlp_b2': _L3_cond_in['mlp_b2']}

def reference(x, cond_1024, mask_BxSxSx11_ik0, L1_cond_Wc, L1_cond_bc, L1_cond_Wq, L1_cond_bq, L1_cond_Wk, L1_cond_bk, L1_cond_Wv, L1_cond_bv, L1_cond_Wo, L1_cond_bo, L1_cond_W1, L1_cond_b1, L1_cond_W2, L1_cond_b2, L2_cond_W_self, L2_cond_b_self, L2_cond_w_bias, L2_cond_b_bias, L2_cond_Wq, L2_cond_bq, L2_cond_Wk, L2_cond_bk, L2_cond_Wout, L2_cond_bout, L3_cond_norm1_w, L3_cond_film1_w, L3_cond_film1_b, L3_cond_q_w, L3_cond_q_b, L3_cond_k_w, L3_cond_k_b, L3_cond_v_w, L3_cond_v_b, L3_cond_proj_w, L3_cond_proj_b, L3_cond_norm2_w, L3_cond_film2_w, L3_cond_film2_b, L3_cond_mlp_w1, L3_cond_mlp_b1, L3_cond_mlp_w2, L3_cond_mlp_b2):
    import jax
    import jax.numpy as jnp

    def _L0_cond_ref(x, r, u):
        import jax, jax.numpy as jnp
        import numpy as np
        N, HW, C = (32, 512, 128)
        WRS_RATIO = 0.5
        P = 0.9
        M = int(WRS_RATIO * C)
        xt = jnp.swapaxes(x, 1, 2)
        score = jnp.mean(xt, axis=2)
        key = r ** (1.0 / score)
        thr = jnp.sort(key, axis=1)[:, C - M][:, None]
        sel = key >= thr
        sel_score = jnp.sum(jnp.where(sel, score, 0.0), axis=1, keepdims=True)
        alpha = jnp.sum(score, axis=1, keepdims=True) / sel_score
        rng = u < P
        maskf = (sel & rng).astype(x.dtype) * alpha
        out = xt * maskf[:, :, None]
        return jnp.swapaxes(out, 1, 2)

    def _L1_cond_ref(x, c, Wc, bc, Wq, bq, Wk, bk, Wv, bv, Wo, bo, W1, b1, W2, b2):
        import jax, jax.numpy as jnp
        import numpy as np
        H = 128
        NH = 16
        DH = H // NH
        MLP = 4 * H
        EPS = 1e-05

        def _ln(x):
            m = jnp.mean(x, axis=-1, keepdims=True)
            v = jnp.mean((x - m) ** 2, axis=-1, keepdims=True)
            return (x - m) * jax.lax.rsqrt(v + EPS)

        def _modulate(x, shift, scale):
            return x * (1.0 + scale[:, None, :]) + shift[:, None, :]
        B, S, _ = x.shape
        c6 = jax.nn.silu(c) @ Wc + bc
        sh_msa, sc_msa, g_msa, sh_mlp, sc_mlp, g_mlp = jnp.split(c6, 6, axis=-1)
        xm = _modulate(_ln(x), sh_msa, sc_msa)
        q = (xm @ Wq + bq).reshape(B, S, NH, DH)
        k = (xm @ Wk + bk).reshape(B, S, NH, DH)
        v = (xm @ Wv + bv).reshape(B, S, NH, DH)
        q = q / DH
        w = jnp.einsum('bqhc,bkhc->bhqk', q, k)
        w = jax.nn.softmax(w, axis=-1)
        y = jnp.einsum('bhqk,bkhc->bqhc', w, v).reshape(B, S, H)
        x = x + g_msa[:, None, :] * (y @ Wo + bo)
        xm2 = _modulate(_ln(x), sh_mlp, sc_mlp)
        h = jax.nn.gelu(xm2 @ W1 + b1, approximate=False)
        x = x + g_mlp[:, None, :] * (h @ W2 + b2)
        return x

    def _L2_cond_ref(v, q, adj, W_self, b_self, w_bias, b_bias, Wq, bq, Wk, bk, Wout, bout):
        import jax, jax.numpy as jnp
        import numpy as np
        NONGT = 20
        H = 16
        NEG = -9000000000000000.0

        def _gat_attention(self_feat, cond_adj, label_bias, Wq, bq, Wk, bk, Wout, bout):
            B, N, F = self_feat.shape
            ng = min(NONGT, N)
            dh = F // H
            kv = self_feat[:, :ng]
            qh = (self_feat @ Wq.T + bq).reshape(B, N, H, dh)
            kh = (kv @ Wk.T + bk).reshape(B, ng, H, dh)
            aff = jnp.einsum('bnhd,bmhd->bnhm', qh, kh) * (1.0 / np.sqrt(dh))
            mask = cond_adj[:, :, None, :] > 0
            aff = jnp.where(mask, aff, NEG) + label_bias[:, :, None, :]
            w = jax.nn.softmax(aff, axis=-1)
            out_t = jnp.einsum('bnhm,bmf->bnhf', w, kv)
            out = jnp.einsum('bnhf,hgf->bnhg', out_t, Wout) + bout.reshape(H, F // H)
            return out.reshape(B, N, F)

        def _forward(v, q, adj, W_self, b_self, w_bias, b_bias, Wq, bq, Wk, bk, Wout, bout):
            adj_f = adj.astype(jnp.float32)
            exp_v = v
            row_zero = exp_v.sum(-1) == 0
            q_exp = jnp.where(row_zero[..., None], 0.0, q[:, None, :])
            vcq = jnp.concatenate([exp_v, q_exp], axis=-1)
            self_feat = vcq @ W_self.T + b_self
            output = self_feat
            for d in range(2):
                A = adj_f if d == 0 else jnp.swapaxes(adj_f, 1, 2)
                A = A[:, :, :NONGT, :]
                cond = A.sum(-1)
                vb = A @ w_bias + b_bias
                output = output + _gat_attention(self_feat, cond, vb, Wq[d], bq[d], Wk[d], bk[d], Wout[d], bout[d])
            rel = jax.nn.relu(output)
            return exp_v + rel
        return _forward(v, q, adj, W_self, b_self, w_bias, b_bias, Wq, bq, Wk, bk, Wout, bout)

    def _L3_cond_ref(x, cond, norm1_w, film1_w, film1_b, q_w, q_b, k_w, k_b, v_w, v_b, proj_w, proj_b, norm2_w, film2_w, film2_b, mlp_w1, mlp_b1, mlp_w2, mlp_b2):
        import jax, jax.numpy as jnp
        import numpy as np
        DIM = 128
        MLP_RATIO = 4
        EPS = 1e-06

        def rmsnorm(x, w):
            return x * jax.lax.rsqrt(jnp.mean(x * x, axis=-1, keepdims=True) + EPS) * w

        def film(x, cond, w, b):
            ss = cond @ w + b
            scale, shift = jnp.split(ss, 2, axis=-1)
            return x * (1.0 + scale[:, None, :]) + shift[:, None, :]
        B, N, D = x.shape
        x_in = x
        h = film(rmsnorm(x, norm1_w), cond, film1_w, film1_b)
        Q = h @ q_w + q_b
        K = h @ k_w + k_b
        V = h @ v_w + v_b
        scores = jnp.einsum('bnd,bmd->bnm', Q, K) * D ** (-0.5)
        attn = jax.nn.softmax(scores, axis=-1)
        out = jnp.einsum('bnm,bmd->bnd', attn, V)
        x = x_in + (out @ proj_w + proj_b)
        x_in = x
        h = film(rmsnorm(x, norm2_w), cond, film2_w, film2_b)
        h = jax.nn.gelu(h @ mlp_w1 + mlp_b1, approximate=False) @ mlp_w2 + mlp_b2
        return x_in + h
    x = _L0_cond_ref(x, cond_1024, cond_1024)
    x = _L1_cond_ref(x, cond_1024, L1_cond_Wc, L1_cond_bc, L1_cond_Wq, L1_cond_bq, L1_cond_Wk, L1_cond_bk, L1_cond_Wv, L1_cond_bv, L1_cond_Wo, L1_cond_bo, L1_cond_W1, L1_cond_b1, L1_cond_W2, L1_cond_b2)
    x = _L2_cond_ref(x, cond_1024, mask_BxSxSx11_ik0, L2_cond_W_self, L2_cond_b_self, L2_cond_w_bias, L2_cond_b_bias, L2_cond_Wq, L2_cond_bq, L2_cond_Wk, L2_cond_bk, L2_cond_Wout, L2_cond_bout)
    x = _L3_cond_ref(x, cond_1024, L3_cond_norm1_w, L3_cond_film1_w, L3_cond_film1_b, L3_cond_q_w, L3_cond_q_b, L3_cond_k_w, L3_cond_k_b, L3_cond_v_w, L3_cond_v_b, L3_cond_proj_w, L3_cond_proj_b, L3_cond_norm2_w, L3_cond_film2_w, L3_cond_film2_b, L3_cond_mlp_w1, L3_cond_mlp_b1, L3_cond_mlp_w2, L3_cond_mlp_b2)
    return x

_drawn_inputs = setup_inputs


def setup_inputs(seed=0):
    import zlib

    import numpy as np

    out = dict(_drawn_inputs(seed))
    spreads = {'L1_cond_bc': (0.0, 0.1),
     'L1_cond_bq': (0.0, 0.8),
     'L1_cond_bk': (0.0, 0.8),
     'L1_cond_bv': (0.0, 0.1),
     'L1_cond_bo': (0.0, 0.1),
     'L1_cond_b1': (0.0, 0.333),
     'L1_cond_b2': (0.0, 0.1),
     'L2_cond_b_self': (0.0, 0.1),
     'L2_cond_bq': (0.0, 0.1),
     'L2_cond_bk': (0.0, 0.1),
     'L2_cond_bout': (0.0, 0.1),
     'L3_cond_norm1_w': (1.0, 0.2),
     'L3_cond_film1_b': (0.0, 0.1),
     'L3_cond_q_b': (0.0, 0.8),
     'L3_cond_k_b': (0.0, 0.8),
     'L3_cond_v_b': (0.0, 0.1),
     'L3_cond_proj_b': (0.0, 0.1),
     'L3_cond_norm2_w': (1.0, 0.2),
     'L3_cond_film2_b': (0.0, 0.1),
     'L3_cond_mlp_b1': (0.0, 0.1),
     'L3_cond_mlp_b2': (0.0, 0.1)}
    factors = {'L1_cond_Wq': 3.53, 'L1_cond_Wk': 3.404}
    for name, (base, spread) in spreads.items():
        noise = np.random.default_rng([zlib.crc32(name.encode()), seed]).standard_normal(out[name].shape)
        drawn = base * np.exp(spread * noise) if base else spread * noise
        out[name] = jnp.asarray(drawn.astype(out[name].dtype))
    for name, factor in factors.items():
        out[name] = (out[name] * factor).astype(out[name].dtype)
    return out
```

```python
from contextlib import ExitStack

import numpy as np

import concourse.bass as bass
from concourse import mybir

F32 = mybir.dt.float32
I32 = mybir.dt.int32
ALU = mybir.AluOpType
ACT = mybir.ActivationFunctionType
AX = mybir.AxisListType

B, S, D = 32, 32, 128
P = 128
BT = P // S
NT = B // BT
NC = 2
T = NT // NC
CB = T * BT
CW = T * P
NH, DH = 16, 8
J, R = 4, 4
MLP = 4
NONGT = 20
NL = 11
VW = R * DH + R
NEG = -9000000000000000.0
LN_EPS, RMS_EPS = 1e-5, 1e-6
LN_MIN = 2.0 ** -64
LOG_TINY, LOG_HUGE = -103.97, 88.8
KEEP = 0.9
TOPK = D // 2

COLS = {}
for _name, _n in (("bc", 6), ("bq1", 1), ("bk1", 1), ("bv1", 1), ("bo1", 1), ("b11", 4), ("b21", 1),
                  ("bself", 1), ("bq2", 2), ("bk2", 2), ("n1w", 1), ("f1b", 2), ("bq3", 1), ("bk3", 1),
                  ("bv3", 1), ("n2w", 1), ("f2b", 2), ("b13", 4), ("b23", 1)):
    COLS[_name] = (sum(n for _, n in COLS.values()), _n)
NCOL = sum(n for _, n in COLS.values())

def _places(parts):
    at, out = 0, {}
    for name, n in parts:
        out[name] = at
        at += n
    return out, at


W1AT, W1N = _places((("wc", 6 * D), ("wq", D), ("wk", D), ("wv", D), ("wo", D), ("w1", MLP * D), ("w2", MLP * D)))
W2AT, W2N = _places((("wsv", D), ("wsq", D), ("wq", 2 * D), ("wk", 2 * D), ("wv", 2 * D)))
W3AT, W3N = _places((("film1", 2 * D), ("wq", D), ("wk", D), ("wvT", D), ("wp", D), ("film2", 2 * D),
                     ("w1", MLP * D), ("w2", MLP * D)))
CAT, CN = _places((("ident", P), ("sel", NT * B), ("rmask", R)))


def build(nc, x, cond, condT, adj, cols, w1, w2, w3, consts, selT_d, rows, wb, out):
    ctx = ExitStack()
    with ctx:
        def sb(name, shape, dt=F32):
            return ctx.enter_context(nc.sbuf_tensor(name, shape, dt))

        def sem(name):
            return ctx.enter_context(nc.semaphore(name))

        def sems(name):
            return [sem(f"{name}{c}") for c in range(NC)]

        def per_chunk(name, shape, dt=F32):
            return [sb(f"{name}{c}", shape, dt) for c in range(NC)]

        bank = [[ctx.enter_context(nc.psum_tensor(f"bank{c}_{i}", [P, CW], F32)) for i in range(4)]
                for c in range(NC)]

        cst = sb("cst", [P, CN])
        ident = cst[:, CAT["ident"]:CAT["ident"] + P]
        sel = cst[:, CAT["sel"]:CAT["sel"] + NT * B].rearrange("p (t b) -> p t b", t=NT)
        rmask = cst[:, CAT["rmask"]:CAT["rmask"] + R]
        selT = sb("selT", [B, NT * P])
        col = sb("col", [P, NCOL])
        w1s = sb("w1s", [P, W1N])
        w2s = sb("w2s", [P, W2N])
        w3s = sb("w3s", [P, W3N])
        rowb = sb("rowb", [P, 3, D])
        wbb = sb("wbb", [P, NL + 1])
        condr = sb("condr", [B, D])
        condc = sb("condc", [P, B])
        adjs = sb("adjs", [P, NT, S * NL], I32)
        elab = sb("elab", [P, 2, T, S])
        edges = sb("edges", [P, NT, S])
        ebias = sb("ebias", [P, NT, S])
        edgef = sb("edgef", [P, NT, S])
        score = sb("score", [B, D])
        iscore = sb("iscore", [B, D])
        rclip = sb("rclip", [B, D])
        lnr = sb("lnr", [B, D])
        rzero = sb("rzero", [B, D])
        logk = sb("logk", [B, D])
        work = sb("work", [B, D])
        top8 = sb("top8", [B, 8])
        selsc = sb("selsc", [B, D])
        sums = sb("sums", [B, 4])
        keepc = sb("keepc", [B, D])
        cmask = sb("cmask", [B, D])
        negc = sb("negc", [P, B])
        expc = sb("expc", [P, B])
        siluc = sb("siluc", [P, B])
        mods = sb("mods", [P, 6, B])
        films = sb("films", [P, 4, B])
        bqs = sb("bqs", [P, 4])
        ones32 = sb("ones32", [P, B])
        half = sb("half", [P, T])
        qself = sb("qself", [B, D])
        wvp = sb("wvp", [P, D])
        bvp = sb("bvp", [P, D])
        bv3b = sb("bv3b", [P, P])
        bout = sb("bout", [P, D])

        xin = per_chunk("xin", [P, T, D])
        xres = per_chunk("xres", [P, T, D])
        st = per_chunk("st", [P, T, 6])
        mv = per_chunk("mv", [P, T, 2])
        var = per_chunk("var", [P, T])
        rstd = per_chunk("rstd", [P, T])
        xn = per_chunk("xn", [P, T, D])
        xm = per_chunk("xm", [P, CW])
        qT = [per_chunk(f"qT{a}_", [P, CW]) for a in range(2)]
        kT = [per_chunk(f"kT{a}_", [P, CW]) for a in range(2)]
        vS = [per_chunk(f"vS{a}_", [P, T, D]) for a in range(2)]
        kx = [per_chunk("kx0_", [P, CB, R, S]), per_chunk("kx1_", [P, CB, R, NONGT])]
        vb = [per_chunk(f"vb{a}_", [P, T, BT, J, VW]) for a in range(2)]
        pr = per_chunk("pr", [P, J, T, R, S])
        pr2 = per_chunk("pr2", [P, J, T, R, S])
        mx = per_chunk("mx", [P, J, T * R])
        pT = [kx[0][c][:, :, :, :].rearrange("p (j b) r k -> p j (b r k)", j=J) for c in range(NC)]
        rs = per_chunk("rs", [P, 2, T * 2 * R])
        y = [per_chunk(f"y{a}_", [P, T, 2, 2, R * DH]) for a in range(2)]
        yT = [xn[c][:, :, :].rearrange("p t d -> p (t d)") for c in range(NC)]
        hid = [pr[c][:, :, :, :, :].rearrange("p i t r k -> p i (t r k)") for c in range(NC)]
        zsel = [xin[c][0:B, :, :].rearrange("p t d -> p (t d)") for c in range(NC)]
        edgeb = per_chunk("edgeb", [P, 2, T, S])
        s3 = per_chunk("s3", [P, T, S])
        mx3 = per_chunk("mx3", [P, T])
        sm3 = per_chunk("sm3", [P, T])
        p3 = per_chunk("p3", [P, T, BT, S])
        v3 = vS[0]

        ld_x = sems("ld_x")
        ld_cond, ld_const, ld_w1, ld_w2, ld_w3, ld_adj = (sem(n) for n in (
            "ld_cond", "ld_const", "ld_w1", "ld_w2", "ld_w3", "ld_adj"))
        (const_set, score_mm, score_in, clip_set, ln_done, keys_done, l0_chain, mask_done, negexp,
         silu_chain, silu_done, mods_mm, mods_done, pool_chain, edges_done, l3w_mm, l3w_done,
         qself_mm, qself_done, bqs_done, films_mm, bias_done) = (sem(n) for n in (
             "const_set", "score_mm", "score_in", "clip_set", "ln_done", "keys_done", "l0_chain",
             "mask_done", "negexp", "silu_chain", "silu_done", "mods_mm", "mods_done", "pool_chain",
             "edges_done", "l3w_mm", "l3w_done", "qself_mm", "qself_done", "bqs_done", "films_mm",
             "bias_done"))
        (mask_mm, x_ready, stats, aggr, rstd_done, xn_done, xt_done, mod_half, xm_done, qkv_mm, q_in,
         k_in, v_in, kx_done, vb_done, logits, biased, max_done, sub_done, exp_done, pt_mm, pt_in,
         pv_mm, rs_done, y_done, yt_mm, yt_in, wo_mm, gate_done, gt_mm, up_mm, gelu_done, down_mm,
         x1t_mm, x1t_in, rowsum_mm, z_done, self_mm, self_in, eb_done, ysum, selft_mm, rel_done,
         sc3_mm, mx3_done, sub3, exp3, sum3, nrm3, pt3_done, y3_mm, stored) = (sems(n) for n in (
             "mask_mm", "x_ready", "stats", "aggr", "rstd_done", "xn_done", "xt_done", "mod_half",
             "xm_done", "qkv_mm", "q_in", "k_in", "v_in", "kx_done", "vb_done", "logits", "biased",
             "max_done", "sub_done", "exp_done", "pt_mm", "pt_in", "pv_mm", "rs_done", "y_done",
             "yt_mm", "yt_in", "wo_mm", "gate_done", "gt_mm", "up_mm", "gelu_done", "down_mm",
             "x1t_mm", "x1t_in", "rowsum_mm", "z_done", "self_mm", "self_in", "eb_done", "ysum",
             "selft_mm", "rel_done", "sc3_mm", "mx3_done", "sub3", "exp3", "sum3", "nrm3",
             "pt3_done", "y3_mm", "stored"))

        def colof(name, i=0):
            at = COLS[name][0] + i
            return col[:, at:at + 1]

        def keys_of(a):
            return S if a == 0 else NONGT

        def buf(a):
            return 0 if a in (0, 1) else 1

        CH = range(NC)
        block = ctx.enter_context(nc.Block())

        @block.sync
        def _(sp):
            xv = x.rearrange("(t p) d -> p t d", p=P)
            for c in CH:
                sp.dma_start(xin[c][:, :, :], xv[:, T * c:T * c + T, :]).then_inc(ld_x[c], 16)
            sp.dma_start(w1s[:, :], w1).then_inc(ld_w1, 16)
            sp.dma_start(w2s[:, :], w2).then_inc(ld_w2, 16)
            sp.dma_start(w3s[:, :], w3).then_inc(ld_w3, 16)
            sp.dma_start(rowb[:, :, :].rearrange("p a d -> p (a d)"),
                         rows.partition_broadcast(P)).then_inc(ld_w3, 16)
            ov = out.rearrange("(t p) d -> p t d", p=P)
            for c in CH:
                sp.wait_ge(x_ready[c], 6)
                sp.dma_start(ov[:, T * c:T * c + T, :], xres[c][:, :, :]).then_inc(stored[c], 16)
            for c in CH:
                sp.wait_ge(stored[c], 16)

        @block.gpsimd
        def _(pool):
            steps = [0]

            def chain(ins):
                steps[0] += 1
                ins.then_inc(pool_chain, 1)
                pool.wait_ge(pool_chain, steps[0])

            for c in CH:
                for a in range(2):
                    chain(pool.memset(vb[a][c][:, :, :, :, :], 0.0))
                    chain(pool.memset(pr2[c][:, :, :, :, NONGT:], 0.0) if a == 0
                          else pool.memset(p3[c][:, :, :, :], 0.0))
                    for r in range(R):
                        chain(pool.memset(vb[a][c][S * r:S * r + S, :, :, :, R * DH + r], 1.0))
            chain(pool.memset(ones32[:, :], 1.0))
            pool.memset(half[:, :], -0.5).then_inc(const_set, 1)
            pool.wait_ge(const_set, 1)

            pool.wait_ge(ld_const, 48)
            pool.tensor_scalar(bqs[:, 0:1], colof("bq1"), 1.0 / DH, None, ALU.mult)
            pool.tensor_scalar(bqs[:, 1:2], colof("bq2", 0), DH ** -0.5, None, ALU.mult)
            pool.tensor_scalar(bqs[:, 2:3], colof("bq2", 1), DH ** -0.5, None, ALU.mult)
            pool.tensor_scalar(bqs[:, 3:4], colof("bq3"), D ** -0.5, None, ALU.mult).then_inc(bqs_done, 1)

            pool.wait_ge(ld_adj, 32)
            lab = adjs[:, :, :].rearrange("p t (s l) -> p t s l", l=NL)
            for c in CH:
                tc = slice(T * c, T * c + T)
                for l in range(NL):
                    chain(pool.tensor_copy(elab[:, 0, :, :], lab[:, tc, :, l]))
                    chain(pool.tensor_scalar(elab[:, 1, :, :], elab[:, 0, :, :], wbb[:, l:l + 1], None, ALU.mult))
                    if l == 0:
                        pool.tensor_copy(edges[:, tc, :], elab[:, 0, :, :])
                        chain(pool.tensor_scalar(ebias[:, tc, :], elab[:, 1, :, :], wbb[:, NL:NL + 1], None, ALU.add))
                    else:
                        pool.tensor_tensor(edges[:, tc, :], edges[:, tc, :], elab[:, 0, :, :], ALU.add)
                        chain(pool.tensor_tensor(ebias[:, tc, :], ebias[:, tc, :], elab[:, 1, :, :], ALU.add))
                chain(pool.tensor_scalar(edges[:, tc, :], edges[:, tc, :], 0.0, NEG, ALU.is_le, ALU.mult))
                pool.tensor_tensor(edgef[:, tc, :], edges[:, tc, :], ebias[:, tc, :], ALU.add)\
                    .then_inc(edges_done, 1)

            def inverse_root(n, c):
                pool.wait_ge(aggr[c], n + 1)
                if n < 2:
                    chain(pool.tensor_scalar(var[c][:, :], mv[c][:, :, 1], LN_EPS, None, ALU.add))
                else:
                    chain(pool.tensor_tensor(var[c][:, :], mv[c][:, :, 0], mv[c][:, :, 0], ALU.mult))
                    chain(pool.tensor_tensor(var[c][:, :], var[c][:, :], mv[c][:, :, 1], ALU.add))
                    chain(pool.tensor_scalar(var[c][:, :], var[c][:, :], RMS_EPS, None, ALU.add))
                pool.tensor_tensor(rstd[c][:, :], var[c][:, :], half[:, :], ALU.pow).then_inc(rstd_done[c], 1)

            for c in CH:
                inverse_root(0, c)
            for c in CH:
                inverse_root(1, c)
            pool.wait_ge(ld_w3, 32)
            chain(pool.tensor_tensor(bout[:, :], rowb[:, 0, :], rowb[:, 1, :], ALU.add))
            for c in CH:
                pool.wait_ge(y_done[c], 4)
                v0 = y[0][c][:, :, :, :, :].rearrange("p t h j d -> p t (h j d)")
                bb = bout[:, :].unsqueeze(1).to_broadcast([P, T, D])
                chain(pool.tensor_tensor(v0, v0, bb, ALU.add))
                pool.wait_ge(y_done[c], 6)
                f0 = y[0][c][:, :, :, :, :].rearrange("p t h j d -> p (t h j d)")
                f1 = y[1][c][:, :, :, :, :].rearrange("p t h j d -> p (t h j d)")
                pool.tensor_tensor(f0, f0, f1, ALU.add).then_inc(ysum[c], 1)
            for n in (2, 3):
                for c in CH:
                    inverse_root(n, c)

        @block.scalar
        def _(act):
            act.dma_start(condr[:, :], cond).then_inc(ld_cond, 16)
            act.dma_start(condc[:, :], condT).then_inc(ld_cond, 16)
            act.dma_start(cst[:, :], consts).then_inc(ld_const, 16)
            act.dma_start(col[:, :], cols).then_inc(ld_const, 16)
            act.dma_start(selT[:, :], selT_d).then_inc(ld_const, 16)
            act.dma_start(adjs[:, :, :], adj.rearrange("(t p) e -> p t e", p=P)).then_inc(ld_adj, 16)
            act.dma_start(wbb[:, :], wb.partition_broadcast(P)).then_inc(ld_adj, 16)

            act.wait_ge(clip_set, 1)
            act.activation(lnr[:, :], rclip[:, :], ACT.Ln).then_inc(ln_done, 1)
            act.wait_ge(ld_cond, 32)
            act.activation(expc[:, :], condc[:, :], ACT.Exp, scale=-1.0).then_inc(negexp, 1)

            def evac_qkv(a, c):
                i, n = buf(a), a
                sc = (1.0 / DH, DH ** -0.5, DH ** -0.5, D ** -0.5)[a]
                act.wait_ge(qkv_mm[c], 3 * n + 1)
                act.activation(qT[i][c][:, :], bank[c][1][:, :], ACT.Identity,
                               bias=bqs[:, a:a + 1], scale=sc).then_inc(q_in[c], 1)
                act.wait_ge(qkv_mm[c], 3 * n + 2)
                kb = (colof("bk1"), colof("bk2", 0), colof("bk2", 1), colof("bk3"))[a]
                kw = CB * (S if a in (0, 3) else NONGT)
                act.activation(kT[i][c][:, 0:kw], bank[c][2][:, 0:kw], ACT.Identity,
                               bias=kb).then_inc(k_in[c], 1)
                if a < 3:
                    act.wait_ge(qkv_mm[c], 3 * n + 3)
                    act.activation(vS[i][c][:, :, :].rearrange("p t d -> p (t d)"), bank[c][3][:, :],
                                   ACT.Copy).then_inc(v_in[c], 1)

            def softmax(a, c):
                w = pr if a == 0 else pr2
                kn = keys_of(a)

                def copy(j):
                    act.wait_ge(pt_mm[c], 4 * a + j + 1)
                    act.activation(pT[c][:, j, :], bank[c][j][:, :], ACT.Copy).then_inc(pt_in[c], 1)

                for j in range(J):
                    act.wait_ge(sub_done[c], 4 * a + j + 1)
                    v = w[c][:, j, :, :, 0:kn].rearrange("p t r k -> p (t r) k")
                    act.activation(v, v, ACT.Exp).then_inc(exp_done[c], 1)
                    if j >= 2:
                        copy(j - 2)
                copy(J - 2)
                copy(J - 1)

            def gelus(m, c):
                name = ("b11", "b13")[m]
                for i in range(MLP):
                    act.wait_ge(up_mm[c], MLP * m + i + 1)
                    act.activation(hid[c][:, i, :], bank[c][(i + 1) % 4][:, :], ACT.Gelu,
                                   bias=colof(name, i)).then_inc(gelu_done[c], 1)

            act.wait_ge(bqs_done, 1)
            for c in CH:
                evac_qkv(0, c)
            for c in CH:
                softmax(0, c)
            for c in CH:
                act.wait_ge(yt_mm[c], 1)
                act.activation(yT[c], bank[c][2][:, :], ACT.Identity, bias=colof("bv1"))\
                    .then_inc(yt_in[c], 1)
            for c in CH:
                gelus(0, c)
            for c in CH:
                act.wait_ge(x1t_mm[c], 1)
                act.activation(xm[c][:, :], bank[c][0][:, :], ACT.Copy).then_inc(x1t_in[c], 1)
            for c in CH:
                act.wait_ge(self_mm[c], 1)
                act.activation(xm[c][:, :], bank[c][2][:, :], ACT.Identity, bias=colof("bself"))\
                    .then_inc(self_in[c], 1)
            for a in (1, 2):
                for c in CH:
                    evac_qkv(a, c)
            for a in (1, 2):
                for c in CH:
                    softmax(a, c)
            for c in CH:
                evac_qkv(3, c)
            for c in CH:
                act.wait_ge(sub3[c], 1)
                act.activation(s3[c][:, :, :], s3[c][:, :, :], ACT.Exp).then_inc(exp3[c], 1)
            for c in CH:
                gelus(1, c)
            for c in CH:
                act.wait_ge(down_mm[c], 2)
                act.activation(yT[c], bank[c][1][:, :], ACT.Identity, bias=colof("b23"))\
                    .then_inc(yt_in[c], 1)

        @block.vector
        def _(dve):
            count = [0]

            def chain(ins):
                count[0] += 1
                ins.then_inc(l0_chain, 1)
                dve.wait_ge(l0_chain, count[0])

            dve.wait_ge(ld_cond, 32)
            dve.tensor_scalar(rclip[:, :], condr[:, :], LN_MIN, None, ALU.max).then_inc(clip_set, 1)
            dve.tensor_scalar(rzero[:, :], condr[:, :], LN_MIN, -1e30, ALU.is_lt, ALU.mult)
            dve.tensor_scalar(keepc[:, :], condr[:, :], KEEP, None, ALU.is_lt)
            dve.wait_ge(score_mm, 1)
            dve.tensor_scalar(score[:, :], bank[0][0][0:B, 0:D], 1.0 / S, None, ALU.mult).then_inc(score_in, 1)
            dve.wait_ge(score_in, 1)
            chain(dve.reciprocal(iscore[:, :], score[:, :]))
            dve.wait_ge(ln_done, 1)
            chain(dve.tensor_tensor(lnr[:, :], lnr[:, :], rzero[:, :], ALU.add))
            chain(dve.tensor_tensor(logk[:, :], lnr[:, :], iscore[:, :], ALU.mult))
            chain(dve.tensor_scalar(logk[:, :], logk[:, :], LOG_TINY, LOG_HUGE, ALU.max, ALU.min))
            for i in range(TOPK // 8):
                src = logk if i == 0 else work
                chain(dve.max(top8[:, :], src[:, :]))
                if i < TOPK // 8 - 1:
                    chain(dve.match_replace(work[:, :], top8[:, :], src[:, :], -3e38))
            thr = top8[:, 7:8]
            dve.tensor_reduce(sums[:, 0:1], score[:, :], AX.X, ALU.add)
            chain(dve.scalar_tensor_tensor(out=selsc[:, :], in0=logk[:, :], scalar=thr, in1=score[:, :],
                                           op0=ALU.is_ge, op1=ALU.mult))
            dve.scalar_tensor_tensor(out=cmask[:, :], in0=logk[:, :], scalar=thr, in1=keepc[:, :],
                                     op0=ALU.is_ge, op1=ALU.mult)
            chain(dve.tensor_reduce(sums[:, 1:2], selsc[:, :], AX.X, ALU.add))
            chain(dve.reciprocal(sums[:, 2:3], sums[:, 1:2]))
            chain(dve.tensor_tensor(sums[:, 3:4], sums[:, 0:1], sums[:, 2:3], ALU.mult))
            dve.tensor_scalar(cmask[:, :], cmask[:, :], sums[:, 3:4], None, ALU.mult).then_inc(mask_done, 1)
            dve.wait_ge(negexp, 1)
            chain(dve.tensor_scalar(expc[:, :], expc[:, :], 1.0, None, ALU.add))
            chain(dve.reciprocal(expc[:, :], expc[:, :]))
            dve.tensor_tensor(siluc[:, :], expc[:, :], condc[:, :], ALU.mult).then_inc(silu_done, 1)

            def normalise(n, c):
                dve.wait_ge(x_ready[c], (1, 2, 4, 5)[n])
                for t in range(T):
                    last = dve.bn_stats(st[c][:, t, :], xres[c][:, t, :])
                last.then_inc(stats[c], 1)
                dve.wait_ge(stats[c], n + 1)
                for t in range(T):
                    last = dve.bn_aggr(mv[c][:, t, :], st[c][:, t, :])
                last.then_inc(aggr[c], 1)

            def apply_norm(n, c):
                dve.wait_ge(rstd_done[c], n + 1)
                for t in range(T):
                    if n < 2:
                        last = dve.tensor_scalar(xn[c][:, t, :], xres[c][:, t, :], mv[c][:, t, 0:1],
                                                 rstd[c][:, t:t + 1], ALU.subtract, ALU.mult)
                    else:
                        last = dve.tensor_scalar(xn[c][:, t, :], xres[c][:, t, :], rstd[c][:, t:t + 1],
                                                 None, ALU.mult)
                last.then_inc(xn_done[c], 1)

            def modulate(n, c):
                scale, shift = ((mods[:, 1, :], mods[:, 0, :]), (mods[:, 4, :], mods[:, 3, :]),
                                (films[:, 0, :], films[:, 1, :]), (films[:, 2, :], films[:, 3, :]))[n]
                mine = slice(CB * c, CB * c + CB)
                xv = xm[c][:, :].rearrange("p (b s) -> p b s", s=S)
                dve.wait_ge(xt_done[c], n + 1)
                dve.tensor_tensor(xv, bank[c][0][:, :].rearrange("p (b s) -> p b s", s=S),
                                  scale[:, mine].unsqueeze(2).to_broadcast([P, CB, S]), ALU.mult)\
                    .then_inc(mod_half[c], 1)
                dve.wait_ge(mod_half[c], n + 1)
                dve.tensor_tensor(xv, xv, shift[:, mine].unsqueeze(2).to_broadcast([P, CB, S]), ALU.add)\
                    .then_inc(xm_done[c], 1)

            def expand(a, c):
                i, kn = buf(a), keys_of(a)
                dve.wait_ge(k_in[c], a + 1)
                for r in range(R):
                    last = dve.tensor_scalar(kx[i][c][:, :, r, 0:kn],
                                             kT[i][c][:, 0:CB * kn].rearrange("p (b k) -> p b k", k=kn),
                                             rmask[:, r:r + 1], None, ALU.mult)
                last.then_inc(kx_done[c], 1)
                dve.wait_ge(v_in[c], a + 1)
                for b4 in range(BT):
                    for r in range(R):
                        src = vS[i][c][S * b4:S * b4 + S, :, :].rearrange("p t (j d) -> p t j d", j=J)
                        last = dve.tensor_copy(vb[i][c][S * r:S * r + S, :, b4, :, DH * r:DH * r + DH],
                                               src[:, :, :, DH * r:DH * r + DH])
                last.then_inc(vb_done[c], 1)

            def subtract_max(a, c):
                w, kn = (pr if a == 0 else pr2), keys_of(a)

                def psum(j):
                    return bank[c][j][:, 0:T * R * kn].rearrange("p (g k) -> p g k", k=kn)

                def wgt(j):
                    return w[c][:, j, :, :, 0:kn].rearrange("p t r k -> p (t r) k")

                def bias(j):
                    dve.wait_ge(logits[c], 4 * a + j + 1)
                    eb = edgeb[c][:, a - 1, :, 0:kn].unsqueeze(2).to_broadcast([P, T, R, kn])
                    dve.tensor_tensor(w[c][:, j, :, :, 0:kn],
                                      bank[c][j][:, 0:T * R * kn].rearrange("p (t r k) -> p t r k", t=T, r=R),
                                      eb, ALU.add).then_inc(biased[c], 1)

                def largest(j):
                    if a == 0:
                        dve.wait_ge(logits[c], 4 * a + j + 1)
                    else:
                        dve.wait_ge(biased[c], 4 * (a - 1) + j + 1)
                    dve.tensor_reduce(mx[c][:, j, :], psum(j) if a == 0 else wgt(j), AX.X, ALU.max)\
                        .then_inc(max_done[c], 1)

                def less(j):
                    dve.wait_ge(max_done[c], 4 * a + j + 1)
                    dve.tensor_tensor(wgt(j), psum(j) if a == 0 else wgt(j),
                                      mx[c][:, j, :].unsqueeze(2).to_broadcast([P, T * R, kn]),
                                      ALU.subtract).then_inc(sub_done[c], 1)

                for j in range(J + 2):
                    if a > 0 and j < J:
                        bias(j)
                    if 1 <= j <= J:
                        largest(j - 1)
                    if j >= 2:
                        less(j - 2)

            def outputs(a, c):
                for h in range(2):
                    n = 2 * a + h + 1
                    pv = bank[c][h][:, 0:T * 2 * VW].rearrange("p (g w) -> p g w", w=VW)
                    dve.wait_ge(pv_mm[c], n)
                    dve.reciprocal(rs[c][:, h, :].rearrange("p (g r) -> p g r", r=R),
                                   pv[:, :, R * DH:VW]).then_inc(rs_done[c], 1)
                    dve.wait_ge(rs_done[c], n)
                    yv = y[buf(a)][c][:, :, h, :, :].rearrange("p t j (r d) -> p t j r d", d=DH)
                    rv = rs[c][:, h, :].rearrange("p (t j r o) -> p t j r o", t=T, j=2, o=1)\
                        .to_broadcast([P, T, 2, R, DH])
                    dve.tensor_tensor(yv, pv[:, :, 0:R * DH].rearrange("p (t j) (r d) -> p t j r d", t=T, d=DH),
                                      rv, ALU.mult).then_inc(y_done[c], 1)

            def gate(m, c):
                src, name, k = ((bank[c][3], "bo1", 2), (bank[c][1], "b21", 5))[m]
                dve.wait_ge((wo_mm, down_mm)[m][c], 1)
                g = mods[:, k, CB * c:CB * c + CB].unsqueeze(2).to_broadcast([P, CB, S])
                dve.scalar_tensor_tensor(out=xm[c][:, :].rearrange("p (b s) -> p b s", s=S),
                                         in0=src[:, :].rearrange("p (b s) -> p b s", s=S),
                                         scalar=colof(name), in1=g, op0=ALU.add, op1=ALU.mult)\
                    .then_inc(gate_done[c], 1)

            def residual(n, src, done, at, c):
                dve.wait_ge(done[c], at)
                dve.tensor_tensor(xres[c][:, :, :], src[c].rearrange("p (t d) -> p t d", d=D),
                                  xres[c][:, :, :], ALU.add).then_inc(x_ready[c], 1)

            bank_of = [[bank[c][i][:, :] for c in CH] for i in range(4)]

            dve.wait_ge(mods_mm, 1)
            for k in range(6):
                last = dve.tensor_scalar(mods[:, k, :], bank[1][0][:, B * k:B * k + B], colof("bc", k),
                                         1.0 if k in (1, 4) else 0.0, ALU.add, ALU.add)
            for k in range(4):
                b = colof(("f1b", "f2b")[k // 2], k % 2)
                src = bank[1][0][:, B * (6 + k):B * (6 + k) + B]
                last = dve.tensor_scalar(films[:, k, :], src, b, 1.0 if k % 2 == 0 else 0.0, ALU.add, ALU.add)
            chain(last)
            dve.tensor_scalar(films[:, 0, :], films[:, 0, :], colof("n1w"), None, ALU.mult)
            dve.tensor_scalar(films[:, 2, :], films[:, 2, :], colof("n2w"), None, ALU.mult)\
                .then_inc(mods_done, 1)
            dve.wait_ge(mods_done, 1)

            for c in CH:
                dve.wait_ge(mask_mm[c], 1)
                dve.tensor_tensor(xres[c][:, :, :], bank[c][3][:, :].rearrange("p (t d) -> p t d", d=D),
                                  xin[c][:, :, :], ALU.mult).then_inc(x_ready[c], 1)
            dve.wait_ge(l3w_mm, 1)
            dve.tensor_copy(bv3b[:, :], colof("bv3").to_broadcast([P, P])).then_inc(bias_done, 1)
            dve.tensor_copy(wvp[:, :], bank[0][2][:, 0:D])
            dve.tensor_copy(qself[:, :], bank[0][2][0:B, D:2 * D]).then_inc(l3w_done, 1)
            for c in CH:
                normalise(0, c)
            for c in CH:
                apply_norm(0, c)
            for c in CH:
                modulate(0, c)
            for c in CH:
                expand(0, c)
            for c in CH:
                subtract_max(0, c)
            for c in CH:
                outputs(0, c)
            for c in CH:
                gate(0, c)
            for c in CH:
                residual(1, bank_of[0], gt_mm, 1, c)
            for c in CH:
                normalise(1, c)
            for c in CH:
                apply_norm(1, c)
            for c in CH:
                modulate(1, c)
            for c in CH:
                dve.wait_ge(edges_done, c + 1)
                e = edgef[:, T * c:T * c + T, :]
                dve.tensor_copy(edgeb[c][:, 0, :, :], e)
                dve.transpose(edgeb[c][:, 1, :, :], e).then_inc(eb_done[c], 1)
            dve.wait_ge(l3w_mm, 2)
            dve.wait_ge(ld_w3, 32)
            dve.tensor_tensor(bvp[:, :], bank[0][3][:, 0:D], rowb[:, 2, :], ALU.add).then_inc(l3w_done, 1)
            for c in CH:
                gate(1, c)
            for c in CH:
                residual(2, bank_of[0], gt_mm, 2, c)
            for c in CH:
                dve.wait_ge(rowsum_mm[c], 1)
                dve.scalar_tensor_tensor(out=zsel[c], in0=bank[c][1][0:B, :], scalar=0.0,
                                         in1=selT[:, CW * c:CW * c + CW], op0=ALU.not_equal,
                                         op1=ALU.mult).then_inc(z_done[c], 1)
            for a in (1, 2):
                for c in CH:
                    expand(a, c)
            for a in (1, 2):
                for c in CH:
                    dve.wait_ge(eb_done[c], 1)
                    subtract_max(a, c)
                for c in CH:
                    outputs(a, c)
            for c in CH:
                dve.wait_ge(selft_mm[c], 1)
                dve.wait_ge(ysum[c], 1)
                dve.tensor_tensor(xn[c][:, :, :].rearrange("p t d -> p (t d)"), bank[c][2][:, :],
                                  y[0][c][:, :, :, :, :].rearrange("p t h j d -> p (t h j d)"),
                                  ALU.add).then_inc(rel_done[c], 1)
                dve.wait_ge(rel_done[c], 1)
                dve.scalar_tensor_tensor(out=xres[c][:, :, :], in0=xn[c][:, :, :], scalar=0.0,
                                         in1=xres[c][:, :, :], op0=ALU.max, op1=ALU.add)\
                    .then_inc(x_ready[c], 1)
            for c in CH:
                normalise(2, c)
            for c in CH:
                apply_norm(2, c)
            for c in CH:
                modulate(2, c)
            for c in CH:
                dve.wait_ge(qkv_mm[c], 12)
                dve.wait_ge(l3w_done, 2)
                dve.tensor_tensor(v3[c][:, :, :], bank[c][3][:, :].rearrange("p (t d) -> p t d", d=D),
                                  bvp[:, :].unsqueeze(1).to_broadcast([P, T, D]), ALU.add)\
                    .then_inc(v_in[c], 1)
            for c in CH:
                sc = bank[c][0][:, 0:T * S].rearrange("p (t k) -> p t k", k=S)
                dve.wait_ge(sc3_mm[c], 1)
                dve.tensor_reduce(mx3[c][:, :], sc, AX.X, ALU.max).then_inc(mx3_done[c], 1)
                dve.wait_ge(mx3_done[c], 1)
                dve.tensor_tensor(s3[c][:, :, :], sc, mx3[c][:, :].unsqueeze(2).to_broadcast([P, T, S]),
                                  ALU.subtract).then_inc(sub3[c], 1)
            for c in CH:
                dve.wait_ge(exp3[c], 1)
                dve.tensor_reduce(sm3[c][:, :], s3[c][:, :, :], AX.X, ALU.add).then_inc(sum3[c], 1)
                dve.wait_ge(sum3[c], 1)
                dve.reciprocal(sm3[c][:, :], sm3[c][:, :]).then_inc(sum3[c], 1)
                dve.wait_ge(sum3[c], 2)
                dve.tensor_tensor(s3[c][:, :, :], s3[c][:, :, :],
                                  sm3[c][:, :].unsqueeze(2).to_broadcast([P, T, S]), ALU.mult)\
                    .then_inc(nrm3[c], 1)
                dve.wait_ge(nrm3[c], 1)
                for b4 in range(BT):
                    rows4 = slice(S * b4, S * b4 + S)
                    last = dve.transpose(p3[c][rows4, :, b4, :], s3[c][rows4, :, :])
                last.then_inc(pt3_done[c], 1)
            for c in CH:
                residual(4, bank_of[1], y3_mm, 1, c)
            for c in CH:
                normalise(3, c)
            for c in CH:
                apply_norm(3, c)
            for c in CH:
                modulate(3, c)
            for c in CH:
                residual(5, bank_of[0], gt_mm, 3, c)

        @block.tensor
        def _(pe):
            def w1of(name, i=0, n=D):
                return w1s[:, W1AT[name] + i * D:W1AT[name] + i * D + n]

            def w2of(name, i=0):
                return w2s[:, W2AT[name] + i * D:W2AT[name] + i * D + D]

            def w3of(name, i=0):
                return w3s[:, W3AT[name] + i * D:W3AT[name] + i * D + D]

            def turn(dst, src, c):
                for t in range(T):
                    last = pe.transpose(dst[:, P * t:P * t + P], src(t), ident)
                return last

            pe.wait_ge(ld_const, 48)
            for t in range(NT):
                if t % T == 0:
                    pe.wait_ge(ld_x[t // T], 16)
                last = pe.matmul(bank[0][0][0:B, 0:D], sel[:, t, :], xin[t // T][:, t % T, :],
                                 start=(t == 0), stop=(t == NT - 1))
            last.then_inc(score_mm, 1)
            pe.wait_ge(silu_done, 1)
            pe.wait_ge(ld_w1, 16)
            for k in range(6):
                pe.matmul(bank[1][0][:, B * k:B * k + B], w1of("wc", k), siluc[:, :], start=True, stop=True)
            pe.wait_ge(ld_w3, 32)
            for k in range(4):
                last = pe.matmul(bank[1][0][:, B * (6 + k):B * (7 + k)], w3of(("film1", "film2")[k // 2], k % 2),
                                 condc[:, :], start=True, stop=True)
            last.then_inc(mods_mm, 1)
            pe.wait_ge(mask_done, 1)
            for c in CH:
                for t in range(T):
                    g = T * c + t
                    last = pe.matmul(bank[c][3][:, P * t:P * t + P], selT[:, P * g:P * g + P], cmask[:, :],
                                     start=True, stop=True)
                last.then_inc(mask_mm[c], 1)
            pe.wait_ge(ld_w2, 16)
            pe.matmul(bank[0][2][:, 0:D], w3of("wvT"), w3of("wp"), start=True, stop=True)
            pe.matmul(bank[0][2][0:B, D:2 * D], condc[:, :], w2of("wsq"), start=True, stop=True)\
                .then_inc(l3w_mm, 1)

            def xn_turn(n, c):
                pe.wait_ge(xn_done[c], n + 1)
                turn(bank[c][0], lambda t: xn[c][:, t, :], c).then_inc(xt_done[c], 1)

            def qkv(a, c):
                if a == 0:
                    src, wq, wk, wv = xm[c], w1of("wq"), w1of("wk"), w1of("wv")
                    pe.wait_ge(xm_done[c], 1)
                elif a < 3:
                    src, wq, wk, wv = xm[c], w2of("wq", a - 1), w2of("wk", a - 1), w2of("wv", a - 1)
                    pe.wait_ge(self_in[c], 1)
                    if a == 2:
                        pe.wait_ge(q_in[c], a)
                else:
                    src, wq, wk, wv = xm[c], w3of("wq"), w3of("wk"), wvp[:, :]
                    pe.wait_ge(xm_done[c], 3)
                    pe.wait_ge(l3w_done, 1)
                pe.matmul(bank[c][1][:, :], wq, src[:, :], start=True, stop=True).then_inc(qkv_mm[c], 1)
                kn = S if a in (0, 3) else NONGT
                if a == 2:
                    pe.wait_ge(k_in[c], a)
                pe.matmul(bank[c][2][:, 0:CB * kn], wk,
                          src[:, :].rearrange("p (b s) -> p b s", s=S)[:, :, 0:kn],
                          start=True, stop=True).then_inc(qkv_mm[c], 1)
                if a == 2:
                    pe.wait_ge(v_in[c], a)
                for t in range(T):
                    last = pe.matmul(bank[c][3][:, P * t:P * t + P], src[:, P * t:P * t + P], wv,
                                     start=True, stop=True)
                last.then_inc(qkv_mm[c], 1)

            def scores(a, c):
                i, kn = buf(a), keys_of(a)
                pe.wait_ge(kx_done[c], a + 1)
                pe.wait_ge(q_in[c], a + 1)
                pe.wait_ge(v_in[c], a + 1)
                if a == 1:
                    pe.wait_ge(q_in[c], 3)
                    pe.wait_ge(k_in[c], 3)
                    pe.wait_ge(v_in[c], 3)
                if a == 2:
                    pe.wait_ge(y_done[c], 4)
                for j in range(J):
                    rows4 = slice(S * j, S * j + S)
                    for t in range(T):
                        for b4 in range(BT):
                            b = BT * t + b4
                            last = pe.matmul(
                                bank[c][j][S * b4:S * b4 + S, R * kn * t:R * kn * (t + 1)],
                                qT[i][c][rows4, S * b:S * b + S],
                                kx[i][c][rows4, b, :, 0:kn], start=True, stop=True)
                    last.then_inc(logits[c], 1)

            def turn_weights(a, c):
                w = pr if a == 0 else pr2
                for j in range(J):
                    pe.wait_ge(exp_done[c], 4 * a + j + 1)
                    turn(bank[c][j], lambda t: w[c][:, j, t, :, :].rearrange("p r k -> p (r k)"), c)\
                        .then_inc(pt_mm[c], 1)

            def values(a, c):
                pe.wait_ge(vb_done[c], a + 1)
                for h in range(2):
                    pe.wait_ge(pt_in[c], 4 * a + 2 * h + 2)
                    for t in range(T):
                        for g in range(2):
                            for b4 in range(BT):
                                j = 2 * h + g
                                at = VW * (2 * t + g)
                                last = pe.matmul(
                                    bank[c][h][S * b4:S * b4 + S, at:at + VW],
                                    pT[c][:, j, P * t + S * b4:P * t + S * b4 + S],
                                    vb[buf(a)][c][:, t, b4, j, :], start=True, stop=True)
                    last.then_inc(pv_mm[c], 1)

            def mlp(m, c):
                w = (w1of, w3of)[m]
                pe.wait_ge(xm_done[c], (2, 4)[m])
                for i in range(MLP):
                    pe.matmul(bank[c][(i + 1) % 4][:, :], w("w1", i), xm[c][:, :], start=True, stop=True)\
                        .then_inc(up_mm[c], 1)

            def mlp_down(m, c):
                w = (w1of, w3of)[m]
                for i in range(MLP):
                    pe.wait_ge(gelu_done[c], MLP * m + i + 1)
                    last = pe.matmul(bank[c][1][:, :], w("w2", i), hid[c][:, i, :],
                                     start=(i == 0), stop=(i == MLP - 1))
                last.then_inc(down_mm[c], 1)

            for c in CH:
                xn_turn(0, c)
            for c in CH:
                qkv(0, c)
            for c in CH:
                scores(0, c)
            for c in CH:
                turn_weights(0, c)
            pe.wait_ge(const_set, 1)
            for c in CH:
                values(0, c)
            for c in CH:
                pe.wait_ge(y_done[c], 2)
                yv = y[0][c]
                turn(bank[c][2], lambda t: yv[:, t, :, :, :].rearrange("p h j d -> p (h j d)"), c)\
                    .then_inc(yt_mm[c], 1)
            for c in CH:
                pe.wait_ge(yt_in[c], 1)
                pe.matmul(bank[c][3][:, :], w1of("wo"), yT[c], start=True, stop=True)\
                    .then_inc(wo_mm[c], 1)
            for c in CH:
                pe.wait_ge(gate_done[c], 1)
                turn(bank[c][0], lambda t: xm[c][:, P * t:P * t + P], c).then_inc(gt_mm[c], 1)
            for c in CH:
                xn_turn(1, c)
            pe.wait_ge(bias_done, 1)
            pe.matmul(bank[0][3][:, 0:D], bv3b[:, :], w3of("wp"), start=True, stop=True).then_inc(l3w_mm, 1)
            pe.wait_ge(l3w_done, 2)
            for c in CH:
                mlp(0, c)
            for c in CH:
                mlp_down(0, c)
            for c in CH:
                pe.wait_ge(gate_done[c], 2)
                turn(bank[c][0], lambda t: xm[c][:, P * t:P * t + P], c).then_inc(gt_mm[c], 1)
            for c in CH:
                pe.wait_ge(x_ready[c], 3)
                turn(bank[c][0], lambda t: xres[c][:, t, :], c).then_inc(x1t_mm[c], 1)
            for c in CH:
                pe.wait_ge(x1t_in[c], 1)
                pe.matmul(bank[c][1][0:B, :], ones32[:, :], xm[c][:, :], start=True, stop=True)\
                    .then_inc(rowsum_mm[c], 1)
            for c in CH:
                pe.matmul(bank[c][2][:, :], w2of("wsv"), xm[c][:, :], start=True, stop=False)
                pe.wait_ge(z_done[c], 1)
                pe.matmul(bank[c][2][:, :], qself[:, :], zsel[c], start=False, stop=True)\
                    .then_inc(self_mm[c], 1)
            for a in (1, 2):
                for c in CH:
                    qkv(a, c)
            for a in (1, 2):
                for c in CH:
                    scores(a, c)
                for c in CH:
                    turn_weights(a, c)
                for c in CH:
                    values(a, c)
            for c in CH:
                pe.wait_ge(pt_in[c], 12)
                turn(bank[c][2], lambda t: xm[c][:, P * t:P * t + P], c).then_inc(selft_mm[c], 1)
            for c in CH:
                xn_turn(2, c)
            for c in CH:
                qkv(3, c)
            for c in CH:
                pe.wait_ge(q_in[c], 4)
                pe.wait_ge(k_in[c], 4)
                for t in range(T):
                    for b4 in range(BT):
                        at = S * (BT * t + b4)
                        last = pe.matmul(bank[c][0][S * b4:S * b4 + S, S * t:S * t + S],
                                         qT[1][c][:, at:at + S], kT[1][c][:, at:at + S],
                                         start=True, stop=True)
                last.then_inc(sc3_mm[c], 1)
            for c in CH:
                pe.wait_ge(pt3_done[c], 1)
                pe.wait_ge(v_in[c], 4)
                for t in range(T):
                    last = pe.matmul(bank[c][1][:, P * t:P * t + P],
                                     p3[c][:, t, :, :].rearrange("p b k -> p (b k)"), v3[c][:, t, :],
                                     start=True, stop=True)
                last.then_inc(y3_mm[c], 1)
            for c in CH:
                xn_turn(3, c)
            for c in CH:
                mlp(1, c)
            for c in CH:
                mlp_down(1, c)
            for c in CH:
                pe.wait_ge(yt_in[c], 2)
                turn(bank[c][0], lambda t: yT[c][:, P * t:P * t + P], c).then_inc(gt_mm[c], 1)


def _layout(a):
    def n(name):
        return np.asarray(a[name])

    def split(w):
        return np.concatenate([w[i:i + D] for i in range(0, w.shape[0], D)], axis=1)

    def cat(*parts):
        return np.ascontiguousarray(np.concatenate(parts, axis=1))

    vectors = ("L1_cond_bc", "L1_cond_bq", "L1_cond_bk", "L1_cond_bv", "L1_cond_bo", "L1_cond_b1",
               "L1_cond_b2", "L2_cond_b_self", "L2_cond_bq", "L2_cond_bk", "L3_cond_norm1_w",
               "L3_cond_film1_b", "L3_cond_q_b", "L3_cond_k_b", "L3_cond_v_b", "L3_cond_norm2_w",
               "L3_cond_film2_b", "L3_cond_mlp_b1", "L3_cond_mlp_b2")
    cols = np.ascontiguousarray(np.concatenate([n(v).reshape(-1, D) for v in vectors]).T)
    wself = n("L2_cond_W_self")
    wq2, wk2, wout = n("L2_cond_Wq"), n("L2_cond_Wk"), n("L2_cond_Wout").reshape(2, D, D)
    w1 = cat(n("L1_cond_Wc"), n("L1_cond_Wq"), n("L1_cond_Wk"), n("L1_cond_Wv"), n("L1_cond_Wo"),
             n("L1_cond_W1"), split(n("L1_cond_W2")))
    w2 = cat(wself[:, :D].T, wself[:, D:].T, wq2[0].T, wq2[1].T, wk2[0].T, wk2[1].T, wout[0].T, wout[1].T)
    w3 = cat(n("L3_cond_film1_w"), n("L3_cond_q_w"), n("L3_cond_k_w"), n("L3_cond_v_w").T,
             n("L3_cond_proj_w"), n("L3_cond_film2_w"), n("L3_cond_mlp_w1"), split(n("L3_cond_mlp_w2")))
    ident = np.eye(P, dtype=np.float32)
    member = np.zeros((B, NT * P), np.float32)
    for b in range(B):
        member[b, S * b:S * b + S] = 1.0
    sel = np.concatenate([member[:, P * t:P * t + P].T for t in range(NT)], axis=1)
    rmask = np.zeros((P, R), np.float32)
    for p in range(P):
        rmask[p, p % (R * DH) // DH] = 1.0
    rows = np.concatenate([n("L2_cond_bout").reshape(-1), n("L3_cond_proj_b")])
    wb = np.concatenate([n("L2_cond_w_bias"), n("L2_cond_b_bias").reshape(1)])
    cond = n("cond_1024")
    return {
        "x": n("x").reshape(B * S, D), "cond": cond, "condT": np.ascontiguousarray(cond.T),
        "adj": n("mask_BxSxSx11_ik0").reshape(B * S, S * NL), "cols": cols, "w1": w1, "w2": w2, "w3": w3,
        "consts": cat(ident, sel, rmask), "selT_d": member, "rows": rows, "wb": wb,
    }


def kernel(**inputs):
    import concourse.bacc as bacc
    from concourse.bass_utils import run_bass_kernel_spmd

    nc = bacc.Bacc("TRN2", target_bir_lowering=False, num_devices=1)
    arrays = _layout(inputs)
    aps = {k: nc.dram_tensor(f"in_{k}", v.shape, mybir.dt.from_np(v.dtype), kind="ExternalInput").ap()
           for k, v in arrays.items()}
    out = nc.dram_tensor("out", (B * S, D), F32, kind="ExternalOutput").ap()
    build(nc, out=out, **aps)
    done = run_bass_kernel_spmd(nc, [{f"in_{k}": v for k, v in arrays.items()}], core_ids=[0])
    return done.results[0]["out"].reshape(B, S, D)
```

```python
from contextlib import ExitStack

import numpy as np

import concourse.bass as bass
from concourse import mybir

F32 = mybir.dt.float32
I32 = mybir.dt.int32
BF16 = mybir.dt.bfloat16
ALU = mybir.AluOpType
ACT = mybir.ActivationFunctionType
AX = mybir.AxisListType

B, S, D = 32, 32, 128
P = 128
BT = P // S
NT = B // BT
NC = 2
T = NT // NC
CB = T * BT
CW = T * P
NH, DH = 16, 8
J, R = 4, 4
MLP = 4
NONGT = 20
NL = 11
VW = R * DH + R
NEG = -9000000000000000.0
LN_EPS, RMS_EPS = 1e-5, 1e-6
LN_MIN = 2.0 ** -64
LOG_TINY, LOG_HUGE = -103.97, 88.8
KEEP = 0.9
PARTS = 3
TOPK = D // 2

ORDER = ("stats0", "apply0", "mod0", "qkv0", "soft0", "turn0", "values0", "yt0", "wo0", "res0",
         "stats1", "apply1", "mod1", "up0", "down0", "res1",
         "x1t", "rowsum", "self", "qkv1", "qkv2", "soft1", "turn1", "values1",
         "soft2", "turn2", "values2", "rel",
         "stats2", "apply2", "mod2", "qkv3", "score3", "y3",
         "stats3", "apply3", "mod3", "up1", "down1")


def schedule():
    return [(name, c) for name in ORDER for c in range(NC)]


COLS = {}
for _name, _n in (("bc", 6), ("bq1", 1), ("bk1", 1), ("bv1", 1), ("bo1", 1), ("b11", 4), ("b21", 1),
                  ("bself", 1), ("bq2", 2), ("bk2", 2), ("n1w", 1), ("f1b", 2), ("bq3", 1), ("bk3", 1),
                  ("bv3", 1), ("n2w", 1), ("f2b", 2), ("b13", 4), ("b23", 1)):
    COLS[_name] = (sum(n for _, n in COLS.values()), _n)
NCOL = sum(n for _, n in COLS.values())

def _places(parts):
    at, out = 0, {}
    for name, n in parts:
        out[name] = at
        at += n
    return out, at


W1AT, W1N = _places((("wc", 6 * D), ("wq", D), ("wk", D), ("wv", D), ("wo", D), ("w1", MLP * D), ("w2", MLP * D)))
W2AT, W2N = _places((("wsv", D), ("wsq", D), ("wq", 2 * D), ("wk", 2 * D), ("wv", 2 * D)))
W3AT, W3N = _places((("film1", 2 * D), ("wq", D), ("wk", D), ("wvT", D), ("wp", D), ("film2", 2 * D),
                     ("w1", MLP * D), ("w2", MLP * D)))
CAT, CN = _places((("ident", P), ("sel", NT * B), ("rmask", R)))


def build(nc, x, cond, condT, adj, cols, w1, w2, w3, consts, selT_d, rows, wb, out):
    ctx = ExitStack()
    with ctx:
        def sb(name, shape, dt=F32):
            return ctx.enter_context(nc.sbuf_tensor(name, shape, dt))

        def sem(name):
            return ctx.enter_context(nc.semaphore(name))

        def sems(name):
            return [sem(f"{name}{c}") for c in range(NC)]

        def per_chunk(name, shape, dt=F32):
            return [sb(f"{name}{c}", shape, dt) for c in range(NC)]

        bank = [[ctx.enter_context(nc.psum_tensor(f"bank{c}_{i}", [P, CW], F32)) for i in range(4)]
                for c in range(NC)]

        cst = sb("cst", [P, CN])
        ident = cst[:, CAT["ident"]:CAT["ident"] + P]
        sel = cst[:, CAT["sel"]:CAT["sel"] + NT * B].rearrange("p (t b) -> p t b", t=NT)
        rmask = cst[:, CAT["rmask"]:CAT["rmask"] + R]
        selT = sb("selT", [B, NT * P])
        col = sb("col", [P, NCOL])
        w1s = sb("w1s", [P, W1N])
        w2s = sb("w2s", [P, W2N])
        w3s = sb("w3s", [P, W3N])
        rowb = sb("rowb", [P, 4, D])
        wbb = sb("wbb", [P, NL + 1])
        condr = sb("condr", [B, D])
        condc = sb("condc", [P, B])
        adjs = sb("adjs", [P, NT, S * NL], I32)
        edges = sb("edges", [P, NT, S])
        ebias = sb("ebias", [P, NT, S])
        score = sb("score", [B, D])
        iscore = sb("iscore", [B, D])
        rclip = sb("rclip", [B, D])
        lnr = sb("lnr", [B, D])
        rzero = sb("rzero", [B, D])
        logk = sb("logk", [B, D])
        work = sb("work", [B, D])
        top8 = sb("top8", [B, 8])
        selsc = sb("selsc", [B, D])
        sums = sb("sums", [B, 4])
        keepc = sb("keepc", [B, D])
        cmask = sb("cmask", [B, D])
        selTb = sb("selTb", [PARTS * B, NT * P], BF16)
        cmaskb = sb("cmaskb", [PARTS * B, D], BF16)
        qselfb = sb("qselfb", [PARTS * B, D], BF16)
        rest = sb("rest", [B, 4, D])
        negc = sb("negc", [P, B])
        expc = sb("expc", [P, B])
        siluc = sb("siluc", [P, B])
        mods = sb("mods", [P, 6, B])
        films = sb("films", [P, 4, B])
        bqs = sb("bqs", [P, 4])
        ones96 = sb("ones96", [P, PARTS * B])
        kbias = sb("kbias", [P, 3, R])
        half = sb("half", [P, T])
        qself = sb("qself", [B, D])
        wvp = sb("wvp", [P, D])
        bvp = sb("bvp", [P, D])
        bv3b = sb("bv3b", [P, P])
        bout = sb("bout", [P, D])

        xin = per_chunk("xin", [P, T, D])
        xres = per_chunk("xres", [P, T, D])
        st = per_chunk("st", [P, T, 6])
        mv = per_chunk("mv", [P, T, 2])
        var = per_chunk("var", [P, T])
        rstd = per_chunk("rstd", [P, T])
        xn = per_chunk("xn", [P, T, D])
        xm = per_chunk("xm", [P, CW])
        qT = [per_chunk(f"qT{a}_", [P, CW]) for a in range(2)]
        kT = per_chunk("kT", [P, CW])
        vS = [per_chunk(f"vS{a}_", [P, T, D]) for a in range(2)]
        kx = [per_chunk("kx0_", [P, CB, R, S]), per_chunk("kx1_", [P, CB, R, NONGT])]
        vb = [per_chunk(f"vb{a}_", [P, T, BT, J, VW]) for a in range(2)]
        pr = per_chunk("pr", [P, J, T, R, S])
        pr2 = per_chunk("pr2", [P, J, T, R, S])
        mx = per_chunk("mx", [P, J, T * R])
        pT = [kx[0][c][:, :, :, :].rearrange("p (j b) r k -> p j (b r k)", j=J) for c in range(NC)]
        rs = per_chunk("rs", [P, 2, T * 2 * R])
        y = [per_chunk(f"y{a}_", [P, T, 2, 2, R * DH]) for a in range(2)]
        yT = [xn[c][:, :, :].rearrange("p t d -> p (t d)") for c in range(NC)]
        wlab = [kx[0][c][:, :, :, :].rearrange("p b r k -> p (b r k)")[:, 0:T * S * NL]
                .rearrange("p (g l) -> p g l", l=NL) for c in range(NC)]
        hid = [pr[c][:, :, :, :, :].rearrange("p i t r k -> p i (t r k)") for c in range(NC)]
        zsel = per_chunk("zsel", [PARTS * B, CW], BF16)
        edgeb = per_chunk("edgeb", [P, 2, T, S])
        s3 = per_chunk("s3", [P, T, S])
        mx3 = per_chunk("mx3", [P, T])
        sm3 = per_chunk("sm3", [P, T])
        p3 = per_chunk("p3", [P, T, BT, S])
        v3 = vS[0]

        ld_x = sems("ld_x")
        ld_cond, ld_const, ld_selT, ld_cols, ld_w1, ld_w2, ld_w3, ld_adj = (sem(n) for n in (
            "ld_cond", "ld_const", "ld_selT", "ld_cols", "ld_w1", "ld_w2", "ld_w3", "ld_adj"))
        (const_set, score_mm, score_in, clip_set, ln_done, keys_done, l0_chain, mask_done, negexp,
         silu_done, mods_mm, mods_done, pool_chain, l3w_mm, l3w_done,
         qself_mm, bqs_done, bias_done, part_done) = (sem(n) for n in (
             "const_set", "score_mm", "score_in", "clip_set", "ln_done", "keys_done", "l0_chain",
             "mask_done", "negexp", "silu_done", "mods_mm", "mods_done", "pool_chain",
             "l3w_mm", "l3w_done", "qself_mm", "bqs_done",
             "bias_done", "part_done"))
        (mask_mm, x_ready, stats, aggr, square_done, var_done, rstd_done, xn_done, xt_done, mod_half, xm_done, qkv_mm, q_in,
         k_in, v_in, vb_done, vb_pool, b2_added, logits, biased, max_done, sub_done, exp_done, pt_mm, pt_in,
         pv_mm, rs_done, y_done, yt_mm, yt_in, wo_mm, gate_done, gt_mm, up_mm, gelu_done, down_mm,
         x1t_mm, x1t_in, rowsum_mm, z_done, self_mm, self_in, eb_done, ysum, selft_mm, rel_done,
         sc3_mm, mx3_done, sub3, exp3, sum3, nrm3, pt3_done, y3_mm, stored) = (sems(n) for n in (
             "mask_mm", "x_ready", "stats", "aggr", "square_done", "var_done", "rstd_done", "xn_done", "xt_done", "mod_half",
             "xm_done", "qkv_mm", "q_in", "k_in", "v_in", "vb_done", "vb_pool", "b2_added", "logits", "biased",
             "max_done", "sub_done", "exp_done", "pt_mm", "pt_in", "pv_mm", "rs_done", "y_done",
             "yt_mm", "yt_in", "wo_mm", "gate_done", "gt_mm", "up_mm", "gelu_done", "down_mm",
             "x1t_mm", "x1t_in", "rowsum_mm", "z_done", "self_mm", "self_in", "eb_done", "ysum",
             "selft_mm", "rel_done", "sc3_mm", "mx3_done", "sub3", "exp3", "sum3", "nrm3",
             "pt3_done", "y3_mm", "stored"))

        def colof(name, i=0):
            at = COLS[name][0] + i
            return col[:, at:at + 1]

        def keys_of(a):
            return S if a == 0 else NONGT

        def buf(a):
            return 0 if a in (0, 1) else 1

        def expand_values(eng, a, c, b4, r):
            src = vS[buf(a)][c][S * b4:S * b4 + S, :, :].rearrange("p t (j d) -> p t j d", j=J)
            return eng.tensor_copy(vb[buf(a)][c][S * r:S * r + S, :, b4, :, DH * r:DH * r + DH],
                                   src[:, :, :, DH * r:DH * r + DH])

        DVE_B4, POOL_B4 = (0, 1), (2, 3)
        CH = range(NC)
        block = ctx.enter_context(nc.Block())

        @block.sync
        def _(sp):
            xv = x.rearrange("(t p) d -> p t d", p=P)
            sp.dma_start(cst[:, :], consts).then_inc(ld_const, 16)
            for c in CH:
                sp.dma_start(xin[c][:, :, :], xv[:, T * c:T * c + T, :]).then_inc(ld_x[c], 16)
            sp.dma_start(selT[:, :], selT_d).then_inc(ld_selT, 16)
            sp.dma_start(w1s[:, :], w1).then_inc(ld_w1, 16)
            sp.dma_start(w3s[:, :], w3).then_inc(ld_w3, 16)
            sp.dma_start(adjs[:, :, :], adj.rearrange("(t p) e -> p t e", p=P)).then_inc(ld_adj, 16)
            sp.dma_start(wbb[:, :], wb.partition_broadcast(P)).then_inc(ld_adj, 16)
            sp.dma_start(rowb[:, :, :].rearrange("p a d -> p (a d)"),
                         rows.partition_broadcast(P)).then_inc(ld_w3, 16)
            sp.dma_start(w2s[:, :], w2).then_inc(ld_w2, 16)
            ov = out.rearrange("(t p) d -> p t d", p=P)
            for c in CH:
                sp.wait_ge(x_ready[c], 6)
                sp.dma_start(ov[:, T * c:T * c + T, :], xres[c][:, :, :]).then_inc(stored[c], 16)
            for c in CH:
                sp.wait_ge(stored[c], 16)

        @block.gpsimd
        def _(pool):
            steps = [0]
            copies = [0] * NC

            def chain(ins):
                steps[0] += 1
                ins.then_inc(pool_chain, 1)
                pool.wait_ge(pool_chain, steps[0])

            for c in CH:
                for a in range(2):
                    chain(pool.memset(vb[a][c][:, :, :, :, :], 0.0))
                    chain(pool.memset(pr2[c][:, :, :, :, NONGT:], 0.0) if a == 0
                          else pool.memset(p3[c][:, :, :, :], 0.0))
                    for r in range(R):
                        chain(pool.memset(vb[a][c][S * r:S * r + S, :, :, :, R * DH + r], 1.0))
            chain(pool.memset(ones96[:, :], 1.0))
            pool.memset(half[:, :], -0.5).then_inc(const_set, 1)
            pool.wait_ge(const_set, 1)

            pool.wait_ge(ld_cols, 16)
            pool.wait_ge(ld_const, 16)
            for a, kb in enumerate((colof("bk1"), colof("bk2", 0), colof("bk2", 1))):
                pool.tensor_scalar(kbias[:, a, :], rmask, kb, None, ALU.mult)
            pool.tensor_scalar(bqs[:, 0:1], colof("bq1"), 1.0 / DH, None, ALU.mult)
            pool.tensor_scalar(bqs[:, 1:2], colof("bq2", 0), DH ** -0.5, None, ALU.mult)
            pool.tensor_scalar(bqs[:, 2:3], colof("bq2", 1), DH ** -0.5, None, ALU.mult)
            pool.tensor_scalar(bqs[:, 3:4], colof("bq3"), D ** -0.5, None, ALU.mult).then_inc(bqs_done, 1)

            def inverse_root(n, c):
                pool.wait_ge(var_done[c], n + 1)
                pool.tensor_tensor(rstd[c][:, :], var[c][:, :], half[:, :], ALU.pow).then_inc(rstd_done[c], 1)
                pool.wait_ge(rstd_done[c], n + 1)

            pool.wait_ge(ld_w3, 32)
            chain(pool.tensor_tensor(bout[:, :], rowb[:, 0, :], rowb[:, 1, :], ALU.add))

            def stage(name, c):
                if name in ("stats0", "stats1", "stats2", "stats3"):
                    inverse_root(int(name[-1]), c)
                elif name in ("soft0", "soft1", "soft2"):
                    pool.wait_ge(v_in[c], int(name[-1]) + 1)
                    for b4 in POOL_B4:
                        for r in range(R):
                            done = expand_values(pool, int(name[-1]), c, b4, r)
                            done.then_inc(vb_pool[c], 1)
                            copies[c] += 1
                            pool.wait_ge(vb_pool[c], copies[c])
                elif name == "mod3":
                    pool.wait_ge(xn_done[c], 4)
                    pool.tensor_tensor(xres[c][:, :, :], xres[c][:, :, :],
                                       rowb[:, 3, :].unsqueeze(1).to_broadcast([P, T, D]), ALU.add)\
                        .then_inc(b2_added[c], 1)
                elif name == "values1":
                    pool.wait_ge(y_done[c], 4)
                    v0 = y[0][c][:, :, :, :, :].rearrange("p t h j d -> p t (h j d)")
                    bb = bout[:, :].unsqueeze(1).to_broadcast([P, T, D])
                    pool.tensor_tensor(v0, v0, bb, ALU.add).then_inc(ysum[c], 1)
                    pool.wait_ge(ysum[c], 1)
                elif name == "values2":
                    pool.wait_ge(y_done[c], 6)
                    pool.wait_ge(ysum[c], 1)
                    f0 = y[0][c][:, :, :, :, :].rearrange("p t h j d -> p (t h j d)")
                    f1 = y[1][c][:, :, :, :, :].rearrange("p t h j d -> p (t h j d)")
                    pool.tensor_tensor(f0, f0, f1, ALU.add).then_inc(ysum[c], 1)

            for name, c in schedule():
                stage(name, c)

        @block.scalar
        def _(act):
            act.dma_start(condr[:, :], cond).then_inc(ld_cond, 16)
            act.dma_start(condc[:, :], condT).then_inc(ld_cond, 16)
            act.dma_start(col[:, :], cols).then_inc(ld_cols, 16)

            act.wait_ge(clip_set, 1)
            act.activation(lnr[:, :], rclip[:, :], ACT.Ln).then_inc(ln_done, 1)
            act.wait_ge(ld_cond, 32)
            act.activation(expc[:, :], condc[:, :], ACT.Exp, scale=-1.0).then_inc(negexp, 1)

            def evac_qkv(a, c):
                i, n = buf(a), a
                sc = (1.0 / DH, DH ** -0.5, DH ** -0.5, D ** -0.5)[a]
                act.wait_ge(qkv_mm[c], 3 * n + 1)
                act.activation(qT[i][c][:, :], bank[c][1][:, :], ACT.Identity,
                               bias=bqs[:, a:a + 1], scale=sc).then_inc(q_in[c], 1)
                act.wait_ge(qkv_mm[c], 3 * n + 2)
                if a == 3:
                    act.activation(kT[c][:, :], bank[c][2][:, :], ACT.Identity, bias=colof("bk3"))\
                        .then_inc(k_in[c], 1)
                    return
                kn = keys_of(a)
                for r in range(R):
                    last = act.activation(kx[i][c][:, :, r, 0:kn],
                                          bank[c][2][:, 0:CB * kn].rearrange("p (b k) -> p b k", k=kn),
                                          ACT.Identity, bias=kbias[:, a, r:r + 1], scale=rmask[:, r:r + 1])
                last.then_inc(k_in[c], 1)

            def exponentials(a, c):
                w, kn = (pr if a == 0 else pr2), keys_of(a)
                for j in range(J):
                    act.wait_ge(sub_done[c], 4 * a + j + 1)
                    v = w[c][:, j, :, :, 0:kn].rearrange("p t r k -> p (t r) k")
                    act.activation(v, v, ACT.Exp).then_inc(exp_done[c], 1)

            def evac_weights(a, c):
                for j in range(J):
                    act.wait_ge(pt_mm[c], 4 * a + j + 1)
                    act.activation(pT[c][:, j, :], bank[c][j][:, :], ACT.Copy).then_inc(pt_in[c], 1)

            def gelus(m, c):
                name = ("b11", "b13")[m]
                for i in range(MLP):
                    act.wait_ge(up_mm[c], MLP * m + i + 1)
                    act.activation(hid[c][:, i, :], bank[c][(i + 1) % 4][:, :], ACT.Gelu,
                                   bias=colof(name, i)).then_inc(gelu_done[c], 1)

            act.wait_ge(bqs_done, 1)

            def stage(name, c):
                if name in ("qkv0", "qkv1", "qkv2", "qkv3"):
                    evac_qkv(int(name[-1]), c)
                elif name in ("soft0", "soft1", "soft2"):
                    exponentials(int(name[-1]), c)
                elif name in ("turn0", "turn1", "turn2"):
                    evac_weights(int(name[-1]), c)
                elif name == "yt0":
                    act.wait_ge(yt_mm[c], 1)
                    act.activation(yT[c], bank[c][2][:, :], ACT.Identity, bias=colof("bv1"))\
                        .then_inc(yt_in[c], 1)
                elif name in ("up0", "up1"):
                    gelus(int(name[-1]), c)
                elif name == "x1t":
                    act.wait_ge(x1t_mm[c], 1)
                    act.activation(xm[c][:, :], bank[c][0][:, :], ACT.Copy).then_inc(x1t_in[c], 1)
                elif name == "self":
                    act.wait_ge(self_mm[c], 1)
                    act.activation(xm[c][:, :], bank[c][2][:, :], ACT.Identity, bias=colof("bself"))\
                        .then_inc(self_in[c], 1)
                elif name == "score3":
                    act.wait_ge(sub3[c], 1)
                    act.activation(s3[c][:, :, :], s3[c][:, :, :], ACT.Exp).then_inc(exp3[c], 1)

            for name, c in schedule():
                stage(name, c)

        @block.vector
        def _(dve):
            count = [0]

            def chain(ins):
                count[0] += 1
                ins.then_inc(l0_chain, 1)
                dve.wait_ge(l0_chain, count[0])

            def edge_bias(c):
                tc = slice(T * c, T * c + T)
                lab = adjs[:, tc, :].rearrange("p t (s l) -> p (t s) l", l=NL)
                e = edges[:, tc, :].rearrange("p t s -> p (t s)")
                eb = ebias[:, tc, :].rearrange("p t s -> p (t s)")
                dve.tensor_tensor(wlab[c], lab, wbb[:, 0:NL].unsqueeze(1).to_broadcast([P, T * S, NL]), ALU.mult)
                chain(dve.tensor_reduce(e, lab, AX.X, ALU.add))
                dve.tensor_reduce(eb, wlab[c], AX.X, ALU.add)
                chain(dve.tensor_scalar(e, e, 0.0, NEG, ALU.is_le, ALU.mult))
                chain(dve.tensor_scalar(eb, eb, wbb[:, NL:NL + 1], None, ALU.add))
                chain(dve.tensor_tensor(edgeb[c][:, 0, :, :], edges[:, tc, :], ebias[:, tc, :], ALU.add))
                dve.transpose(edgeb[c][:, 1, :, :], edgeb[c][:, 0, :, :]).then_inc(eb_done[c], 1)

            def split(dst, src, k, done):
                left = src
                for i in range(PARTS - 1):
                    chain(dve.tensor_copy(dst[B * i:B * i + B, :], left))
                    chain(dve.tensor_copy(rest[:, k + 1, :], dst[B * i:B * i + B, :]))
                    chain(dve.tensor_tensor(rest[:, k, :], left, rest[:, k + 1, :], ALU.subtract))
                    left = rest[:, k, :]
                dve.tensor_copy(dst[B * (PARTS - 1):B * PARTS, :], left).then_inc(done, 1)

            dve.wait_ge(ld_cond, 32)
            dve.tensor_scalar(rclip[:, :], condr[:, :], LN_MIN, None, ALU.max).then_inc(clip_set, 1)
            dve.tensor_scalar(rzero[:, :], condr[:, :], LN_MIN, -1e30, ALU.is_lt, ALU.mult)
            dve.tensor_scalar(keepc[:, :], condr[:, :], KEEP, None, ALU.is_lt)
            dve.wait_ge(ld_selT, 16)
            for i in range(PARTS):
                dve.tensor_copy(selTb[B * i:B * i + B, :], selT[:, :])
            dve.wait_ge(negexp, 1)
            chain(dve.tensor_scalar(expc[:, :], expc[:, :], 1.0, None, ALU.add))
            chain(dve.reciprocal(expc[:, :], expc[:, :]))
            dve.tensor_tensor(siluc[:, :], expc[:, :], condc[:, :], ALU.mult).then_inc(silu_done, 1)
            dve.wait_ge(ld_cols, 16)
            dve.tensor_copy(bv3b[:, :], colof("bv3").to_broadcast([P, P])).then_inc(bias_done, 1)
            dve.wait_ge(score_mm, 1)
            dve.tensor_scalar(score[:, :], bank[0][0][0:B, 0:D], 1.0 / S, None, ALU.mult).then_inc(score_in, 1)
            dve.wait_ge(score_in, 1)
            chain(dve.reciprocal(iscore[:, :], score[:, :]))
            dve.wait_ge(ln_done, 1)
            chain(dve.tensor_tensor(lnr[:, :], lnr[:, :], rzero[:, :], ALU.add))
            chain(dve.tensor_tensor(logk[:, :], lnr[:, :], iscore[:, :], ALU.mult))
            chain(dve.tensor_scalar(logk[:, :], logk[:, :], LOG_TINY, LOG_HUGE, ALU.max, ALU.min))
            for i in range(TOPK // 8):
                src = logk if i == 0 else work
                chain(dve.max(top8[:, :], src[:, :]))
                if i < TOPK // 8 - 1:
                    chain(dve.match_replace(work[:, :], top8[:, :], src[:, :], -3e38))
            thr = top8[:, 7:8]
            dve.tensor_reduce(sums[:, 0:1], score[:, :], AX.X, ALU.add)
            chain(dve.scalar_tensor_tensor(out=selsc[:, :], in0=logk[:, :], scalar=thr, in1=score[:, :],
                                           op0=ALU.is_ge, op1=ALU.mult))
            dve.scalar_tensor_tensor(out=cmask[:, :], in0=logk[:, :], scalar=thr, in1=keepc[:, :],
                                     op0=ALU.is_ge, op1=ALU.mult)
            chain(dve.tensor_reduce(sums[:, 1:2], selsc[:, :], AX.X, ALU.add))
            chain(dve.reciprocal(sums[:, 2:3], sums[:, 1:2]))
            chain(dve.tensor_tensor(sums[:, 3:4], sums[:, 0:1], sums[:, 2:3], ALU.mult))
            chain(dve.tensor_scalar(cmask[:, :], cmask[:, :], sums[:, 3:4], None, ALU.mult))
            split(cmaskb, cmask[:, :], 0, mask_done)

            def normalise(n, c):
                dve.wait_ge(x_ready[c], (1, 2, 4, 5)[n])
                for t in range(T):
                    last = dve.bn_stats(st[c][:, t, :], xres[c][:, t, :])
                last.then_inc(stats[c], 1)
                dve.wait_ge(stats[c], n + 1)
                for t in range(T):
                    last = dve.bn_aggr(mv[c][:, t, :], st[c][:, t, :])
                last.then_inc(aggr[c], 1)
                dve.wait_ge(aggr[c], n + 1)
                if n < 2:
                    dve.tensor_scalar(var[c][:, :], mv[c][:, :, 1], LN_EPS, None, ALU.add)\
                        .then_inc(var_done[c], 1)
                else:
                    dve.tensor_tensor(var[c][:, :], mv[c][:, :, 0], mv[c][:, :, 0], ALU.mult)\
                        .then_inc(square_done[c], 1)
                    dve.wait_ge(square_done[c], n - 1)
                    dve.scalar_tensor_tensor(out=var[c][:, :], in0=mv[c][:, :, 1], scalar=RMS_EPS,
                                             in1=var[c][:, :], op0=ALU.add, op1=ALU.add)\
                        .then_inc(var_done[c], 1)

            def apply_norm(n, c):
                dve.wait_ge(rstd_done[c], n + 1)
                for t in range(T):
                    if n < 2:
                        last = dve.tensor_scalar(xn[c][:, t, :], xres[c][:, t, :], mv[c][:, t, 0:1],
                                                 rstd[c][:, t:t + 1], ALU.subtract, ALU.mult)
                    else:
                        last = dve.tensor_scalar(xn[c][:, t, :], xres[c][:, t, :], rstd[c][:, t:t + 1],
                                                 None, ALU.mult)
                last.then_inc(xn_done[c], 1)

            def modulate(n, c):
                scale, shift = ((mods[:, 1, :], mods[:, 0, :]), (mods[:, 4, :], mods[:, 3, :]),
                                (films[:, 0, :], films[:, 1, :]), (films[:, 2, :], films[:, 3, :]))[n]
                mine = slice(CB * c, CB * c + CB)
                xv = xm[c][:, :].rearrange("p (b s) -> p b s", s=S)
                dve.wait_ge(xt_done[c], n + 1)
                dve.tensor_tensor(xv, bank[c][0][:, :].rearrange("p (b s) -> p b s", s=S),
                                  scale[:, mine].unsqueeze(2).to_broadcast([P, CB, S]), ALU.mult)\
                    .then_inc(mod_half[c], 1)
                dve.wait_ge(mod_half[c], n + 1)
                dve.tensor_tensor(xv, xv, shift[:, mine].unsqueeze(2).to_broadcast([P, CB, S]), ALU.add)\
                    .then_inc(xm_done[c], 1)

            def evac_values(a, c):
                dve.wait_ge(qkv_mm[c], 3 * a + 3)
                dve.tensor_copy(vS[buf(a)][c][:, :, :].rearrange("p t d -> p (t d)"), bank[c][3][:, :])\
                    .then_inc(v_in[c], 1)

            def subtract_max(a, c):
                w, kn = (pr if a == 0 else pr2), keys_of(a)

                def psum(j):
                    return bank[c][j][:, 0:T * R * kn].rearrange("p (g k) -> p g k", k=kn)

                def wgt(j):
                    return w[c][:, j, :, :, 0:kn].rearrange("p t r k -> p (t r) k")

                def bias(j):
                    dve.wait_ge(logits[c], 4 * a + j + 1)
                    eb = edgeb[c][:, a - 1, :, 0:kn].unsqueeze(2).to_broadcast([P, T, R, kn])
                    dve.tensor_tensor(w[c][:, j, :, :, 0:kn],
                                      bank[c][j][:, 0:T * R * kn].rearrange("p (t r k) -> p t r k", t=T, r=R),
                                      eb, ALU.add).then_inc(biased[c], 1)

                def largest(j):
                    if a == 0:
                        dve.wait_ge(logits[c], 4 * a + j + 1)
                    else:
                        dve.wait_ge(biased[c], 4 * (a - 1) + j + 1)
                    dve.tensor_reduce(mx[c][:, j, :], psum(j) if a == 0 else wgt(j), AX.X, ALU.max)\
                        .then_inc(max_done[c], 1)

                def less(j):
                    dve.wait_ge(max_done[c], 4 * a + j + 1)
                    dve.tensor_tensor(wgt(j), psum(j) if a == 0 else wgt(j),
                                      mx[c][:, j, :].unsqueeze(2).to_broadcast([P, T * R, kn]),
                                      ALU.subtract).then_inc(sub_done[c], 1)

                for j in range(J + 2):
                    if a > 0 and j < J:
                        bias(j)
                    if 1 <= j <= J:
                        largest(j - 1)
                    if j >= 2:
                        less(j - 2)
                    if j in DVE_B4:
                        dve.wait_ge(v_in[c], a + 1)
                        for r in range(R):
                            last = expand_values(dve, a, c, j, r)
                        last.then_inc(vb_done[c], 1)

            def outputs(a, c):
                for h in range(2):
                    n = 2 * a + h + 1
                    pv = bank[c][h][:, 0:T * 2 * VW].rearrange("p (g w) -> p g w", w=VW)
                    dve.wait_ge(pv_mm[c], n)
                    dve.reciprocal(rs[c][:, h, :].rearrange("p (g r) -> p g r", r=R),
                                   pv[:, :, R * DH:VW]).then_inc(rs_done[c], 1)
                    dve.wait_ge(rs_done[c], n)
                    yv = y[buf(a)][c][:, :, h, :, :].rearrange("p t j (r d) -> p t j r d", d=DH)
                    rv = rs[c][:, h, :].rearrange("p (t j r o) -> p t j r o", t=T, j=2, o=1)\
                        .to_broadcast([P, T, 2, R, DH])
                    dve.tensor_tensor(yv, pv[:, :, 0:R * DH].rearrange("p (t j) (r d) -> p t j r d", t=T, d=DH),
                                      rv, ALU.mult).then_inc(y_done[c], 1)

            def gate(m, c):
                src, name, k = ((bank[c][3], "bo1", 2), (bank[c][1], "b21", 5))[m]
                dve.wait_ge((wo_mm, down_mm)[m][c], 1)
                g = mods[:, k, CB * c:CB * c + CB].unsqueeze(2).to_broadcast([P, CB, S])
                dve.scalar_tensor_tensor(out=xm[c][:, :].rearrange("p (b s) -> p b s", s=S),
                                         in0=src[:, :].rearrange("p (b s) -> p b s", s=S),
                                         scalar=colof(name), in1=g, op0=ALU.add, op1=ALU.mult)\
                    .then_inc(gate_done[c], 1)

            def residual(n, src, done, at, c):
                dve.wait_ge(done[c], at)
                dve.tensor_tensor(xres[c][:, :, :], src[c].rearrange("p (t d) -> p t d", d=D),
                                  xres[c][:, :, :], ALU.add).then_inc(x_ready[c], 1)

            bank_of = [[bank[c][i][:, :] for c in CH] for i in range(4)]

            dve.wait_ge(mods_mm, 1)
            dve.wait_ge(ld_cols, 16)
            for k in range(6):
                last = dve.tensor_scalar(mods[:, k, :], bank[1][0][:, B * k:B * k + B], colof("bc", k),
                                         1.0 if k in (1, 4) else 0.0, ALU.add, ALU.add)
            for k in range(4):
                b = colof(("f1b", "f2b")[k // 2], k % 2)
                src = bank[1][0][:, B * (6 + k):B * (6 + k) + B]
                last = dve.tensor_scalar(films[:, k, :], src, b, 1.0 if k % 2 == 0 else 0.0, ALU.add, ALU.add)
            chain(last)
            dve.tensor_scalar(films[:, 0, :], films[:, 0, :], colof("n1w"), None, ALU.mult)
            dve.tensor_scalar(films[:, 2, :], films[:, 2, :], colof("n2w"), None, ALU.mult)\
                .then_inc(mods_done, 1)
            dve.wait_ge(mods_done, 1)

            for c in CH:
                dve.wait_ge(mask_mm[c], 1)
                dve.tensor_tensor(xres[c][:, :, :], bank[c][3][:, :].rearrange("p (t d) -> p t d", d=D),
                                  xin[c][:, :, :], ALU.mult).then_inc(x_ready[c], 1)
            def small_weights():
                dve.wait_ge(l3w_mm, 1)
                dve.tensor_copy(wvp[:, :], bank[0][2][:, 0:D])
                dve.tensor_copy(qself[:, :], bank[0][2][0:B, D:2 * D])
                dve.wait_ge(ld_w3, 32)
                dve.tensor_tensor(bvp[:, :], bank[0][2][:, 2 * D:3 * D], rowb[:, 2, :], ALU.add)\
                    .then_inc(l3w_done, 1)
                dve.wait_ge(l3w_done, 1)

            def score3(c):
                sc = bank[c][0][:, 0:T * S].rearrange("p (t k) -> p t k", k=S)
                dve.wait_ge(sc3_mm[c], 1)
                dve.tensor_reduce(mx3[c][:, :], sc, AX.X, ALU.max).then_inc(mx3_done[c], 1)
                dve.wait_ge(mx3_done[c], 1)
                dve.tensor_tensor(s3[c][:, :, :], sc, mx3[c][:, :].unsqueeze(2).to_broadcast([P, T, S]),
                                  ALU.subtract).then_inc(sub3[c], 1)
                dve.wait_ge(exp3[c], 1)
                dve.tensor_reduce(sm3[c][:, :], s3[c][:, :, :], AX.X, ALU.add).then_inc(sum3[c], 1)
                dve.wait_ge(sum3[c], 1)
                dve.reciprocal(sm3[c][:, :], sm3[c][:, :]).then_inc(sum3[c], 1)
                dve.wait_ge(sum3[c], 2)
                dve.tensor_tensor(s3[c][:, :, :], s3[c][:, :, :],
                                  sm3[c][:, :].unsqueeze(2).to_broadcast([P, T, S]), ALU.mult)\
                    .then_inc(nrm3[c], 1)
                dve.wait_ge(nrm3[c], 1)
                for b4 in range(BT):
                    rows4 = slice(S * b4, S * b4 + S)
                    last = dve.transpose(p3[c][rows4, :, b4, :], s3[c][rows4, :, :])
                last.then_inc(pt3_done[c], 1)

            def stage(name, c):
                if name in ("stats0", "stats1", "stats2", "stats3"):
                    normalise(int(name[-1]), c)
                elif name in ("apply0", "apply1", "apply2", "apply3"):
                    apply_norm(int(name[-1]), c)
                elif name in ("mod0", "mod1", "mod2", "mod3"):
                    if (name, c) == ("mod0", 0):
                        small_weights()
                    modulate(int(name[-1]), c)
                elif name in ("qkv0", "qkv1", "qkv2"):
                    evac_values(int(name[-1]), c)
                elif name in ("soft0", "soft1", "soft2"):
                    subtract_max(int(name[-1]), c)
                elif name in ("values0", "values1", "values2"):
                    outputs(int(name[-1]), c)
                elif name == "wo0":
                    gate(0, c)
                elif name == "res0":
                    residual(1, bank_of[0], gt_mm, 1, c)
                elif name == "up0":
                    if c == 0:
                        split(qselfb, qself[:, :], 2, part_done)
                    dve.wait_ge(ld_adj, 32)
                    edge_bias(c)
                elif name == "down0":
                    gate(1, c)
                elif name == "res1":
                    residual(2, bank_of[0], gt_mm, 2, c)
                elif name == "rowsum":
                    dve.wait_ge(rowsum_mm[c], 1)
                    dve.scalar_tensor_tensor(out=zsel[c][:, :], in0=bank[c][1][0:PARTS * B, :], scalar=0.0,
                                             in1=selTb[:, CW * c:CW * c + CW], op0=ALU.not_equal,
                                             op1=ALU.mult).then_inc(z_done[c], 1)
                elif name == "rel":
                    dve.wait_ge(selft_mm[c], 1)
                    dve.wait_ge(ysum[c], 2)
                    dve.tensor_tensor(xn[c][:, :, :].rearrange("p t d -> p (t d)"), bank[c][2][:, :],
                                      y[0][c][:, :, :, :, :].rearrange("p t h j d -> p (t h j d)"),
                                      ALU.add).then_inc(rel_done[c], 1)
                    dve.wait_ge(rel_done[c], 1)
                    dve.scalar_tensor_tensor(out=xres[c][:, :, :], in0=xn[c][:, :, :], scalar=0.0,
                                             in1=xres[c][:, :, :], op0=ALU.max, op1=ALU.add)\
                        .then_inc(x_ready[c], 1)
                elif name == "qkv3":
                    dve.wait_ge(qkv_mm[c], 12)
                    dve.tensor_tensor(v3[c][:, :, :], bank[c][3][:, :].rearrange("p (t d) -> p t d", d=D),
                                      bvp[:, :].unsqueeze(1).to_broadcast([P, T, D]), ALU.add)\
                        .then_inc(v_in[c], 1)
                elif name == "score3":
                    score3(c)
                elif name == "y3":
                    residual(4, bank_of[1], y3_mm, 1, c)
                elif name == "down1":
                    dve.wait_ge(b2_added[c], 1)
                    residual(5, bank_of[1], down_mm, 2, c)

            for name, c in schedule():
                stage(name, c)

        @block.tensor
        def _(pe):
            def w1of(name, i=0, n=D):
                return w1s[:, W1AT[name] + i * D:W1AT[name] + i * D + n]

            def w2of(name, i=0):
                return w2s[:, W2AT[name] + i * D:W2AT[name] + i * D + D]

            def w3of(name, i=0):
                return w3s[:, W3AT[name] + i * D:W3AT[name] + i * D + D]

            def turn(dst, src, c):
                for t in range(T):
                    last = pe.transpose(dst[:, P * t:P * t + P], src(t), ident)
                return last

            pe.wait_ge(ld_const, 16)
            for t in range(NT):
                if t % T == 0:
                    pe.wait_ge(ld_x[t // T], 16)
                last = pe.matmul(bank[0][0][0:B, 0:D], sel[:, t, :], xin[t // T][:, t % T, :],
                                 start=(t == 0), stop=(t == NT - 1))
            last.then_inc(score_mm, 1)
            pe.wait_ge(silu_done, 1)
            pe.wait_ge(ld_w1, 16)
            for k in range(6):
                pe.matmul(bank[1][0][:, B * k:B * k + B], w1of("wc", k), siluc[:, :], start=True, stop=True)
            pe.wait_ge(ld_w3, 32)
            for k in range(4):
                last = pe.matmul(bank[1][0][:, B * (6 + k):B * (7 + k)], w3of(("film1", "film2")[k // 2], k % 2),
                                 condc[:, :], start=True, stop=True)
            last.then_inc(mods_mm, 1)
            pe.wait_ge(mask_done, 1)
            for c in CH:
                for t in range(T):
                    g = T * c + t
                    last = pe.matmul(bank[c][3][:, P * t:P * t + P], selTb[:, P * g:P * g + P], cmaskb[:, :],
                                     start=True, stop=True)
                last.then_inc(mask_mm[c], 1)
            pe.wait_ge(ld_w2, 16)
            pe.matmul(bank[0][2][:, 0:D], w3of("wvT"), w3of("wp"), start=True, stop=True)
            pe.matmul(bank[0][2][0:B, D:2 * D], condc[:, :], w2of("wsq"), start=True, stop=True)
            pe.wait_ge(bias_done, 1)
            pe.matmul(bank[0][2][:, 2 * D:3 * D], bv3b[:, :], w3of("wp"), start=True, stop=True)\
                .then_inc(l3w_mm, 1)

            def xn_turn(n, c):
                pe.wait_ge(xn_done[c], n + 1)
                turn(bank[c][0], lambda t: xn[c][:, t, :], c).then_inc(xt_done[c], 1)

            def qkv(a, c):
                if a == 0:
                    src, wq, wk, wv = xm[c], w1of("wq"), w1of("wk"), w1of("wv")
                    pe.wait_ge(xm_done[c], 1)
                    pe.wait_ge(l3w_done, 1)
                elif a < 3:
                    src, wq, wk, wv = xm[c], w2of("wq", a - 1), w2of("wk", a - 1), w2of("wv", a - 1)
                    pe.wait_ge(self_in[c], 1)
                    if a == 2:
                        pe.wait_ge(q_in[c], a)
                else:
                    src, wq, wk, wv = xm[c], w3of("wq"), w3of("wk"), wvp[:, :]
                    pe.wait_ge(xm_done[c], 3)
                pe.matmul(bank[c][1][:, :], wq, src[:, :], start=True, stop=True).then_inc(qkv_mm[c], 1)
                kn = S if a in (0, 3) else NONGT
                if a == 2:
                    pe.wait_ge(k_in[c], a)
                pe.matmul(bank[c][2][:, 0:CB * kn], wk,
                          src[:, :].rearrange("p (b s) -> p b s", s=S)[:, :, 0:kn],
                          start=True, stop=True).then_inc(qkv_mm[c], 1)
                if a == 2:
                    pe.wait_ge(v_in[c], a)
                for t in range(T):
                    last = pe.matmul(bank[c][3][:, P * t:P * t + P], src[:, P * t:P * t + P], wv,
                                     start=True, stop=True)
                last.then_inc(qkv_mm[c], 1)

            def scores(a, c):
                i, kn = buf(a), keys_of(a)
                pe.wait_ge(k_in[c], a + 1)
                pe.wait_ge(q_in[c], a + 1)
                pe.wait_ge(v_in[c], a + 1)
                if a == 1:
                    pe.wait_ge(q_in[c], 3)
                    pe.wait_ge(k_in[c], 3)
                    pe.wait_ge(v_in[c], 3)
                if a == 2:
                    pe.wait_ge(y_done[c], 4)
                for j in range(J):
                    rows4 = slice(S * j, S * j + S)
                    for t in range(T):
                        for b4 in range(BT):
                            b = BT * t + b4
                            last = pe.matmul(
                                bank[c][j][S * b4:S * b4 + S, R * kn * t:R * kn * (t + 1)],
                                qT[i][c][rows4, S * b:S * b + S],
                                kx[i][c][rows4, b, :, 0:kn], start=True, stop=True)
                    last.then_inc(logits[c], 1)

            def turn_weights(a, c):
                w = pr if a == 0 else pr2
                for j in range(J):
                    pe.wait_ge(exp_done[c], 4 * a + j + 1)
                    turn(bank[c][j], lambda t: w[c][:, j, t, :, :].rearrange("p r k -> p (r k)"), c)\
                        .then_inc(pt_mm[c], 1)

            def values(a, c):
                pe.wait_ge(vb_done[c], len(DVE_B4) * (a + 1))
                pe.wait_ge(vb_pool[c], len(POOL_B4) * R * (a + 1))
                for h in range(2):
                    pe.wait_ge(pt_in[c], 4 * a + 2 * h + 2)
                    for t in range(T):
                        for g in range(2):
                            for b4 in range(BT):
                                j = 2 * h + g
                                at = VW * (2 * t + g)
                                last = pe.matmul(
                                    bank[c][h][S * b4:S * b4 + S, at:at + VW],
                                    pT[c][:, j, P * t + S * b4:P * t + S * b4 + S],
                                    vb[buf(a)][c][:, t, b4, j, :], start=True, stop=True)
                    last.then_inc(pv_mm[c], 1)

            def mlp(m, c):
                w = (w1of, w3of)[m]
                pe.wait_ge(xm_done[c], (2, 4)[m])
                for i in range(MLP):
                    pe.matmul(bank[c][(i + 1) % 4][:, :], w("w1", i), xm[c][:, :], start=True, stop=True)\
                        .then_inc(up_mm[c], 1)

            def mlp_down(m, c):
                w = (w1of, w3of)[m]
                if m == 0:
                    for i in range(MLP):
                        pe.wait_ge(gelu_done[c], MLP * m + i + 1)
                        last = pe.matmul(bank[c][1][:, :], w("w2", i), hid[c][:, i, :],
                                         start=(i == 0), stop=(i == MLP - 1))
                else:
                    pe.wait_ge(gelu_done[c], MLP * (m + 1))
                    for t in range(T):
                        for i in range(MLP):
                            last = pe.matmul(bank[c][1][:, P * t:P * t + P], hid[c][:, i, P * t:P * t + P],
                                             w("w2", i), start=(i == 0), stop=(i == MLP - 1))
                last.then_inc(down_mm[c], 1)

            def stage(name, c):
                if name in ("apply0", "apply1", "apply2", "apply3"):
                    xn_turn(int(name[-1]), c)
                elif name in ("qkv0", "qkv1", "qkv2", "qkv3"):
                    qkv(int(name[-1]), c)
                elif name in ("soft0", "soft1", "soft2"):
                    scores(int(name[-1]), c)
                elif name in ("turn0", "turn1", "turn2"):
                    turn_weights(int(name[-1]), c)
                elif name in ("values0", "values1", "values2"):
                    pe.wait_ge(const_set, 1)
                    values(int(name[-1]), c)
                elif name == "yt0":
                    pe.wait_ge(y_done[c], 2)
                    turn(bank[c][2], lambda t: y[0][c][:, t, :, :, :].rearrange("p h j d -> p (h j d)"), c)\
                        .then_inc(yt_mm[c], 1)
                elif name == "wo0":
                    pe.wait_ge(yt_in[c], 1)
                    pe.matmul(bank[c][3][:, :], w1of("wo"), yT[c], start=True, stop=True)\
                        .then_inc(wo_mm[c], 1)
                elif name in ("res0", "res1"):
                    pe.wait_ge(gate_done[c], 1 + int(name[-1]))
                    turn(bank[c][0], lambda t: xm[c][:, P * t:P * t + P], c).then_inc(gt_mm[c], 1)
                elif name in ("up0", "up1"):
                    mlp(int(name[-1]), c)
                elif name in ("down0", "down1"):
                    mlp_down(int(name[-1]), c)
                elif name == "x1t":
                    pe.wait_ge(x_ready[c], 3)
                    turn(bank[c][0], lambda t: xres[c][:, t, :], c).then_inc(x1t_mm[c], 1)
                elif name == "rowsum":
                    pe.wait_ge(x1t_in[c], 1)
                    pe.matmul(bank[c][1][0:PARTS * B, :], ones96[:, :], xm[c][:, :], start=True, stop=True)\
                        .then_inc(rowsum_mm[c], 1)
                    pe.matmul(bank[c][2][:, :], w2of("wsv"), xm[c][:, :], start=True, stop=False)
                elif name == "self":
                    pe.wait_ge(z_done[c], 1)
                    pe.wait_ge(part_done, 1)
                    pe.matmul(bank[c][2][:, :], qselfb[:, :], zsel[c][:, :], start=False, stop=True)\
                        .then_inc(self_mm[c], 1)
                elif name == "rel":
                    pe.wait_ge(pt_in[c], 12)
                    turn(bank[c][2], lambda t: xm[c][:, P * t:P * t + P], c).then_inc(selft_mm[c], 1)
                elif name == "score3":
                    pe.wait_ge(q_in[c], 4)
                    pe.wait_ge(k_in[c], 4)
                    for t in range(T):
                        for b4 in range(BT):
                            at = S * (BT * t + b4)
                            last = pe.matmul(bank[c][0][S * b4:S * b4 + S, S * t:S * t + S],
                                             qT[1][c][:, at:at + S], kT[c][:, at:at + S],
                                             start=True, stop=True)
                    last.then_inc(sc3_mm[c], 1)
                elif name == "y3":
                    pe.wait_ge(pt3_done[c], 1)
                    pe.wait_ge(v_in[c], 4)
                    for t in range(T):
                        last = pe.matmul(bank[c][1][:, P * t:P * t + P],
                                         p3[c][:, t, :, :].rearrange("p b k -> p (b k)"), v3[c][:, t, :],
                                         start=True, stop=True)
                    last.then_inc(y3_mm[c], 1)

            for name, c in schedule():
                stage(name, c)


def _layout(a):
    def n(name):
        return np.asarray(a[name])

    def split(w):
        return np.concatenate([w[i:i + D] for i in range(0, w.shape[0], D)], axis=1)

    def cat(*parts):
        return np.ascontiguousarray(np.concatenate(parts, axis=1))

    vectors = ("L1_cond_bc", "L1_cond_bq", "L1_cond_bk", "L1_cond_bv", "L1_cond_bo", "L1_cond_b1",
               "L1_cond_b2", "L2_cond_b_self", "L2_cond_bq", "L2_cond_bk", "L3_cond_norm1_w",
               "L3_cond_film1_b", "L3_cond_q_b", "L3_cond_k_b", "L3_cond_v_b", "L3_cond_norm2_w",
               "L3_cond_film2_b", "L3_cond_mlp_b1", "L3_cond_mlp_b2")
    cols = np.ascontiguousarray(np.concatenate([n(v).reshape(-1, D) for v in vectors]).T)
    wself = n("L2_cond_W_self")
    wq2, wk2, wout = n("L2_cond_Wq"), n("L2_cond_Wk"), n("L2_cond_Wout").reshape(2, D, D)
    w1 = cat(n("L1_cond_Wc"), n("L1_cond_Wq"), n("L1_cond_Wk"), n("L1_cond_Wv"), n("L1_cond_Wo"),
             n("L1_cond_W1"), split(n("L1_cond_W2")))
    w2 = cat(wself[:, :D].T, wself[:, D:].T, wq2[0].T, wq2[1].T, wk2[0].T, wk2[1].T, wout[0].T, wout[1].T)
    w3 = cat(n("L3_cond_film1_w"), n("L3_cond_q_w"), n("L3_cond_k_w"), n("L3_cond_v_w").T,
             n("L3_cond_proj_w"), n("L3_cond_film2_w"), n("L3_cond_mlp_w1"), split(n("L3_cond_mlp_w2")))
    ident = np.eye(P, dtype=np.float32)
    member = np.zeros((B, NT * P), np.float32)
    for b in range(B):
        member[b, S * b:S * b + S] = 1.0
    sel = np.concatenate([member[:, P * t:P * t + P].T for t in range(NT)], axis=1)
    rmask = np.zeros((P, R), np.float32)
    for p in range(P):
        rmask[p, p % (R * DH) // DH] = 1.0
    rows = np.concatenate([n("L2_cond_bout").reshape(-1), n("L3_cond_proj_b"), n("L3_cond_mlp_b2")])
    wb = np.concatenate([n("L2_cond_w_bias"), n("L2_cond_b_bias").reshape(1)])
    cond = n("cond_1024")
    return {
        "x": n("x").reshape(B * S, D), "cond": cond, "condT": np.ascontiguousarray(cond.T),
        "adj": n("mask_BxSxSx11_ik0").reshape(B * S, S * NL), "cols": cols, "w1": w1, "w2": w2, "w3": w3,
        "consts": cat(ident, sel, rmask), "selT_d": member, "rows": rows, "wb": wb,
    }


def kernel(**inputs):
    import concourse.bacc as bacc
    from concourse.bass_utils import run_bass_kernel_spmd

    nc = bacc.Bacc("TRN2", target_bir_lowering=False, num_devices=1)
    arrays = _layout(inputs)
    aps = {k: nc.dram_tensor(f"in_{k}", v.shape, mybir.dt.from_np(v.dtype), kind="ExternalInput").ap()
           for k, v in arrays.items()}
    out = nc.dram_tensor("out", (B * S, D), F32, kind="ExternalOutput").ap()
    build(nc, out=out, **aps)
    done = run_bass_kernel_spmd(nc, [{f"in_{k}": v for k, v in arrays.items()}], core_ids=[0])
    return done.results[0]["out"].reshape(B, S, D)
```
